# Optimizing a Trainium2 kernel written in Bass

```python
import numpy as np
import jax
import jax.numpy as jnp

def _softmax(x, axis=-1):
    return jax.nn.softmax(x, axis=axis)

def _gelu(x):
    return jax.nn.gelu(x, approximate=True)

def _silu(x):
    return jax.nn.silu(x)

def _sigmoid(x):
    return jax.nn.sigmoid(x)

def _layernorm(x, axis=-1, eps=1e-05):
    m = jnp.mean(x, axis=axis, keepdims=True)
    v = jnp.var(x, axis=axis, keepdims=True)
    return (x - m) / jnp.sqrt(v + eps)

def _scatter_add(tgt, idx, src, axis=0):
    return tgt.at[idx].add(src)

def _segment_sum(src, seg, n):
    return jax.ops.segment_sum(src, seg, n)
kernel_name = 'mk_cond_seq_d2_seqx_r4_2b03b8'

def setup_inputs(seed: int=0):
    np.random.seed(seed)
    _w = jnp.asarray

    def _rec_inputs():
        import jax
        import jax.numpy as jnp
        _rk = jax.random.key(seed)
        x = -0.0003929 + 0.9999 * jax.random.normal(jax.random.fold_in(_rk, 1), (32, 64, 512), jnp.float32)
        _lenS = 64 - jax.random.randint(jax.random.fold_in(_rk, 7), (32,), 0, max(1, 64 // 4) + 1, jnp.int32)
        _lenS2 = 64 - jax.random.randint(jax.random.fold_in(_rk, 8), (32,), 0, max(1, 64 // 4) + 1, jnp.int32)
        pos_BxS = jnp.broadcast_to(jnp.arange(64, dtype=jnp.int32), (32, 64))
        cond_2048 = 0.00782532 + 1.00527 * jax.random.normal(jax.random.fold_in(_rk, 12), (32, 512), jnp.float32)
        return (x, pos_BxS, cond_2048)
    x, pos_BxS, cond_2048 = _rec_inputs()

    def _L0_cond_setup():
        import jax, jax.numpy as jnp
        import numpy as np
        HIDDEN, NQ, NKV, HD, INTER = (512, 8, 1, 64, 2048)
        B, S = (4, 512)
        EPS = 1e-06
        ROPE_BASE = 10000.0

        def ada_rms(x, t, w, tw):
            n = x * jax.lax.rsqrt(jnp.mean(jnp.square(x), axis=-1, keepdims=True) + EPS)
            scale = t @ tw.T
            return n * (w * (1.0 + scale))[:, None, :]

        def apply_rope(x, pos_ids):
            half = HD // 2
            inv_freq = 1.0 / ROPE_BASE ** (jnp.arange(0, HD, 2, dtype=jnp.float32) / HD)
            ang = pos_ids.astype(jnp.float32)[:, :, None] * inv_freq
            cos = jnp.concatenate([jnp.cos(ang), jnp.cos(ang)], axis=-1)[:, None]
            sin = jnp.concatenate([jnp.sin(ang), jnp.sin(ang)], axis=-1)[:, None]
            x1, x2 = (x[..., :half], x[..., half:])
            rot = jnp.concatenate([-x2, x1], axis=-1)
            return x * cos + rot * sin
        key = jax.random.key(seed)
        ks = jax.random.split(key, 12)
        f32 = jnp.float32
        inp = {'x': jax.random.normal(ks[0], (B, S, HIDDEN), f32), 'pos_ids': jnp.broadcast_to(jnp.arange(S, dtype=jnp.int32), (B, S)), 'time_emb': jax.random.normal(ks[1], (B, HIDDEN), f32), 'ln1_w': jnp.ones((HIDDEN,), f32), 'ln1_tw': jax.random.normal(ks[2], (HIDDEN, HIDDEN), f32) * 0.02, 'ln2_w': jnp.ones((HIDDEN,), f32), 'ln2_tw': jax.random.normal(ks[3], (HIDDEN, HIDDEN), f32) * 0.02, 'Wq': jax.random.normal(ks[4], (NQ * HD, HIDDEN), f32) * 0.02, 'Wk': jax.random.normal(ks[5], (NKV * HD, HIDDEN), f32) * 0.02, 'Wv': jax.random.normal(ks[6], (NKV * HD, HIDDEN), f32) * 0.02, 'Wo': jax.random.normal(ks[7], (HIDDEN, NQ * HD), f32) * 0.02, 'Wg': jax.random.normal(ks[8], (INTER, HIDDEN), f32) * 0.02, 'Wu': jax.random.normal(ks[9], (INTER, HIDDEN), f32) * 0.02, 'Wd': jax.random.normal(ks[10], (HIDDEN, INTER), f32) * 0.02}
        return inp
    _L0_cond_all = _L0_cond_setup()
    _L0_cond_in = {k: v for k, v in _L0_cond_all.items() if k in ('ln1_w', 'ln1_tw', 'ln2_w', 'ln2_tw', 'Wq', 'Wk', 'Wv', 'Wo', 'Wg', 'Wu', 'Wd')}
    del _L0_cond_all

    def _L1_cond_setup():
        import jax, jax.numpy as jnp
        import numpy as np
        D_MODEL = 512
        N_HEADS = 16
        N_KV_HEADS = 4
        HEAD_DIM = D_MODEL // N_HEADS
        N_GROUPS = N_HEADS // N_KV_HEADS
        BLOCK_SIZE = 128
        WINDOW = 64
        GLOBAL_EVERY = 64
        LATENT = 128
        ROPE_THETA = 10000.0
        LN_EPS = 1e-05

        def _rope_tables(T, dtype):
            freqs = 1.0 / ROPE_THETA ** (jnp.arange(0, HEAD_DIM, 2, dtype=jnp.float32) / HEAD_DIM)
            emb = jnp.arange(T, dtype=jnp.float32)[:, None] * freqs[None, :]
            cos = jnp.concatenate([jnp.cos(emb), jnp.cos(emb)], axis=-1).astype(dtype)
            sin = jnp.concatenate([jnp.sin(emb), jnp.sin(emb)], axis=-1).astype(dtype)
            return (cos, sin)

        def _rotate_half(x):
            h = x.shape[-1] // 2
            return jnp.concatenate([-x[..., h:], x[..., :h]], axis=-1)

        def _sparse_mask(T):
            idx = jnp.arange(T)
            blk = idx // BLOCK_SIZE
            future_block = blk[None, :] > blk[:, None]
            outside_window = jnp.abs(idx[None, :] - idx[:, None]) > WINDOW
            global_visible = jnp.broadcast_to((idx % GLOBAL_EVERY == 0)[None, :], (T, T))
            return outside_window & ~global_visible | future_block
        key = jax.random.key(seed)
        ks = jax.random.split(key, 9)
        B, T = (2, 512)
        s = 0.02
        return {'x': jax.random.normal(ks[0], (B, T, D_MODEL), jnp.float32), 't_emb': jax.random.normal(ks[1], (B, D_MODEL), jnp.float32), 'W_ada': jax.random.normal(ks[2], (2 * D_MODEL, D_MODEL), jnp.float32) * s, 'b_ada': jnp.zeros((2 * D_MODEL,), jnp.float32), 'Wq': jax.random.normal(ks[3], (N_HEADS * HEAD_DIM, D_MODEL), jnp.float32) * s, 'Wkd': jax.random.normal(ks[4], (LATENT, D_MODEL), jnp.float32) * s, 'Wku': jax.random.normal(ks[5], (N_KV_HEADS * HEAD_DIM, LATENT), jnp.float32) * s, 'Wvu': jax.random.normal(ks[6], (N_KV_HEADS * HEAD_DIM, LATENT), jnp.float32) * s, 'Wo': jax.random.normal(ks[7], (D_MODEL, N_HEADS * HEAD_DIM), jnp.float32) * s}
    _L1_cond_all = _L1_cond_setup()
    _L1_cond_in = {k: v for k, v in _L1_cond_all.items() if k in ('W_ada', 'b_ada', 'Wq', 'Wkd', 'Wku', 'Wvu', 'Wo')}
    del _L1_cond_all
    return {'x': x, 'pos_BxS': pos_BxS, 'cond_2048': cond_2048, 'L0_cond_ln1_w': _L0_cond_in['ln1_w'], 'L0_cond_ln1_tw': _L0_cond_in['ln1_tw'], 'L0_cond_ln2_w': _L0_cond_in['ln2_w'], 'L0_cond_ln2_tw': _L0_cond_in['ln2_tw'], 'L0_cond_Wq': _L0_cond_in['Wq'], 'L0_cond_Wk': _L0_cond_in['Wk'], 'L0_cond_Wv': _L0_cond_in['Wv'], 'L0_cond_Wo': _L0_cond_in['Wo'], 'L0_cond_Wg': _L0_cond_in['Wg'], 'L0_cond_Wu': _L0_cond_in['Wu'], 'L0_cond_Wd': _L0_cond_in['Wd'], 'L1_cond_W_ada': _L1_cond_in['W_ada'], 'L1_cond_b_ada': _L1_cond_in['b_ada'], 'L1_cond_Wq': _L1_cond_in['Wq'], 'L1_cond_Wkd': _L1_cond_in['Wkd'], 'L1_cond_Wku': _L1_cond_in['Wku'], 'L1_cond_Wvu': _L1_cond_in['Wvu'], 'L1_cond_Wo': _L1_cond_in['Wo']}

def reference(x, pos_BxS, cond_2048, L0_cond_ln1_w, L0_cond_ln1_tw, L0_cond_ln2_w, L0_cond_ln2_tw, L0_cond_Wq, L0_cond_Wk, L0_cond_Wv, L0_cond_Wo, L0_cond_Wg, L0_cond_Wu, L0_cond_Wd, L1_cond_W_ada, L1_cond_b_ada, L1_cond_Wq, L1_cond_Wkd, L1_cond_Wku, L1_cond_Wvu, L1_cond_Wo):
    import jax
    import jax.numpy as jnp

    def _L0_cond_ref(x, pos_ids, time_emb, ln1_w, ln1_tw, ln2_w, ln2_tw, Wq, Wk, Wv, Wo, Wg, Wu, Wd):
        import jax, jax.numpy as jnp
        import numpy as np
        HIDDEN, NQ, NKV, HD, INTER = (512, 8, 1, 64, 2048)
        B, S = (4, 512)
        EPS = 1e-06
        ROPE_BASE = 10000.0

        def ada_rms(x, t, w, tw):
            n = x * jax.lax.rsqrt(jnp.mean(jnp.square(x), axis=-1, keepdims=True) + EPS)
            scale = t @ tw.T
            return n * (w * (1.0 + scale))[:, None, :]

        def apply_rope(x, pos_ids):
            half = HD // 2
            inv_freq = 1.0 / ROPE_BASE ** (jnp.arange(0, HD, 2, dtype=jnp.float32) / HD)
            ang = pos_ids.astype(jnp.float32)[:, :, None] * inv_freq
            cos = jnp.concatenate([jnp.cos(ang), jnp.cos(ang)], axis=-1)[:, None]
            sin = jnp.concatenate([jnp.sin(ang), jnp.sin(ang)], axis=-1)[:, None]
            x1, x2 = (x[..., :half], x[..., half:])
            rot = jnp.concatenate([-x2, x1], axis=-1)
            return x * cos + rot * sin
        b, s, _ = x.shape
        g = NQ // NKV
        res = x
        h = ada_rms(x, time_emb, ln1_w, ln1_tw)
        q = (h @ Wq.T).reshape(b, s, NQ, HD).transpose(0, 2, 1, 3)
        k = (h @ Wk.T).reshape(b, s, NKV, HD).transpose(0, 2, 1, 3)
        v = (h @ Wv.T).reshape(b, s, NKV, HD).transpose(0, 2, 1, 3)
        q = apply_rope(q, pos_ids)
        k = apply_rope(k, pos_ids)
        qg = q.reshape(b, NKV, g, s, HD)
        scores = jnp.einsum('bkgsd,bktd->bkgst', qg, k) / jnp.sqrt(jnp.float32(HD))
        attn = jax.nn.softmax(scores, axis=-1)
        ctx = jnp.einsum('bkgst,bktd->bkgsd', attn, v)
        ctx = ctx.reshape(b, NQ, s, HD).transpose(0, 2, 1, 3).reshape(b, s, NQ * HD)
        x = res + ctx @ Wo.T
        res = x
        h = ada_rms(x, time_emb, ln2_w, ln2_tw)
        mlp = jax.nn.silu(h @ Wg.T) * (h @ Wu.T) @ Wd.T
        return res + mlp

    def _L1_cond_ref(x, t_emb, W_ada, b_ada, Wq, Wkd, Wku, Wvu, Wo):
        import jax, jax.numpy as jnp
        import numpy as np
        D_MODEL = 512
        N_HEADS = 16
        N_KV_HEADS = 4
        HEAD_DIM = D_MODEL // N_HEADS
        N_GROUPS = N_HEADS // N_KV_HEADS
        BLOCK_SIZE = 128
        WINDOW = 64
        GLOBAL_EVERY = 64
        LATENT = 128
        ROPE_THETA = 10000.0
        LN_EPS = 1e-05

        def _rope_tables(T, dtype):
            freqs = 1.0 / ROPE_THETA ** (jnp.arange(0, HEAD_DIM, 2, dtype=jnp.float32) / HEAD_DIM)
            emb = jnp.arange(T, dtype=jnp.float32)[:, None] * freqs[None, :]
            cos = jnp.concatenate([jnp.cos(emb), jnp.cos(emb)], axis=-1).astype(dtype)
            sin = jnp.concatenate([jnp.sin(emb), jnp.sin(emb)], axis=-1).astype(dtype)
            return (cos, sin)

        def _rotate_half(x):
            h = x.shape[-1] // 2
            return jnp.concatenate([-x[..., h:], x[..., :h]], axis=-1)

        def _sparse_mask(T):
            idx = jnp.arange(T)
            blk = idx // BLOCK_SIZE
            future_block = blk[None, :] > blk[:, None]
            outside_window = jnp.abs(idx[None, :] - idx[:, None]) > WINDOW
            global_visible = jnp.broadcast_to((idx % GLOBAL_EVERY == 0)[None, :], (T, T))
            return outside_window & ~global_visible | future_block
        B, T, C = x.shape
        proj = t_emb @ W_ada.T + b_ada
        scale, shift = (proj[:, :C], proj[:, C:])
        mu = jnp.mean(x, axis=-1, keepdims=True)
        var = jnp.mean(jnp.square(x - mu), axis=-1, keepdims=True)
        h = (x - mu) * jax.lax.rsqrt(var + LN_EPS)
        h = h * (1.0 + scale[:, None, :]) + shift[:, None, :]
        q = (h @ Wq.T).reshape(B, T, N_HEADS, HEAD_DIM).transpose(0, 2, 1, 3)
        c_kv = h @ Wkd.T
        k = (c_kv @ Wku.T).reshape(B, T, N_KV_HEADS, HEAD_DIM).transpose(0, 2, 1, 3)
        v = (c_kv @ Wvu.T).reshape(B, T, N_KV_HEADS, HEAD_DIM).transpose(0, 2, 1, 3)
        cos, sin = _rope_tables(T, x.dtype)
        cos, sin = (cos[None, None], sin[None, None])
        q = q * cos + _rotate_half(q) * sin
        k = k * cos + _rotate_half(k) * sin
        k_exp = jnp.repeat(k, N_GROUPS, axis=1)
        v_exp = jnp.repeat(v, N_GROUPS, axis=1)
        mask = _sparse_mask(T)
        scores = jnp.einsum('bhtd,bhsd->bhts', q, k_exp) / jnp.sqrt(jnp.asarray(HEAD_DIM, x.dtype))
        scores = jnp.where(mask[None, None], jnp.asarray(-jnp.inf, x.dtype), scores)
        attn = jax.nn.softmax(scores, axis=-1)
        y = jnp.einsum('bhts,bhsd->bhtd', attn, v_exp)
        out = y.transpose(0, 2, 1, 3).reshape(B, T, C) @ Wo.T
        return x + out
    x = _L0_cond_ref(x, pos_BxS, cond_2048, L0_cond_ln1_w, L0_cond_ln1_tw, L0_cond_ln2_w, L0_cond_ln2_tw, L0_cond_Wq, L0_cond_Wk, L0_cond_Wv, L0_cond_Wo, L0_cond_Wg, L0_cond_Wu, L0_cond_Wd)
    x = _L1_cond_ref(x, cond_2048, L1_cond_W_ada, L1_cond_b_ada, L1_cond_Wq, L1_cond_Wkd, L1_cond_Wku, L1_cond_Wvu, L1_cond_Wo)
    return x

_drawn_inputs = setup_inputs


def setup_inputs(seed=0):
    import zlib

    import numpy as np

    out = dict(_drawn_inputs(seed))
    spreads = {'L0_cond_ln1_w': (1.0, 0.6), 'L0_cond_ln2_w': (1.0, 0.2), 'L1_cond_b_ada': (0.0, 0.8)}
    factors = {'L0_cond_ln1_tw': 4.042,
     'L0_cond_Wq': 6.386,
     'L0_cond_Wk': 6.358,
     'L1_cond_W_ada': 2.734,
     'L1_cond_Wq': 8.0,
     'L1_cond_Wku': 8.0}
    for name, (base, spread) in spreads.items():
        noise = np.random.default_rng([zlib.crc32(name.encode()), seed]).standard_normal(out[name].shape)
        drawn = base * np.exp(spread * noise) if base else spread * noise
        out[name] = jnp.asarray(drawn.astype(out[name].dtype))
    for name, factor in factors.items():
        out[name] = (out[name] * factor).astype(out[name].dtype)
    return out
```

```python
from contextlib import ExitStack

import numpy as np
import concourse.bass as bass
from concourse import mybir

F32 = mybir.dt.float32
F32R = mybir.dt.float32r
I32 = mybir.dt.int32
ALU = mybir.AluOpType
ACT = mybir.ActivationFunctionType
AX_X = mybir.AxisListType.X

P = 128
S = 64
TB_TOKENS = 512


class Tile:

    def __init__(self, n, parity):
        self.n, self.par = n, parity % 2

    def at(self, shift):
        return Tile(self.n + shift, self.par + shift)


def wait(eng, sem, count):
    if isinstance(count, int) and count <= 0:
        return
    eng.wait_ge(sem, count)


def run_tiles(eng, n_tiles, stages):
    low = min(shift for _, shift in stages)
    high = max(shift for _, shift in stages)
    begin, end = -high, n_tiles - low
    loop_from = 2 - low + (2 - low) % 2
    loop_to = n_tiles - high
    loop_to -= loop_to % 2

    def step(t):
        for stage, shift in stages:
            u = t.at(shift)
            if isinstance(u.n, int) and not 0 <= u.n < n_tiles:
                continue
            stage(u)

    for t in range(begin, loop_from):
        step(Tile(t, t))
    with eng.Fori(loop_from // 2, loop_to // 2) as pair:
        for k in range(2):
            step(Tile(pair * 2 + k, k))
    for t in range(loop_to, end):
        step(Tile(t, t))


def build(nc, x, pos, condT, ln1_w, ln1_twT, ln2_w, ln2_twT, WqT, WkT, WvT, WoT, WgT, WuT, WdT,
          adaT, b_ada, Wq1T, WkdT, WkuT, WvuT, Wo1T, invf, rope1, ident, out):
    D = WqT.shape[0]
    KT = D // P
    NTOK = x.shape[0]
    NT = NTOK // P
    NB = NTOK // S
    INTER = WgT.shape[1]
    NG = INTER // P
    NBLK = NTOK // TB_TOKENS
    TPB = TB_TOKENS // P
    HD0, HD1 = WkT.shape[1], 32
    QK0 = (D + 2 * HD0) // 2
    QK1 = (D + P) // 2
    TWO_PI = 2 * np.pi
    C1 = 6.28125
    C2 = float(np.float32(np.round((TWO_PI - C1) * 2.0 ** 21) / 2.0 ** 21))
    C3 = float(np.float32(TWO_PI - C1 - C2))
    ROUND = 12582912.0

    with ExitStack() as ctx:
        def sb(name, shape, dt=F32, into=ctx):
            return into.enter_context(nc.sbuf_tensor(name, shape, dt))

        def sem(name):
            return ctx.enter_context(nc.semaphore(name))

        xres = sb("xres", [P, NT, D])
        wqh, wql = sb("wqh", [P, KT, 2 * QK0], F32R), sb("wql", [P, KT, 2 * QK0], F32R)
        woh, wol = sb("woh", [P, KT, D], F32R), sb("wol", [P, KT, D], F32R)
        kvh, kvl = sb("kvh", [P, 2 * P], F32R), sb("kvl", [P, 2 * P], F32R)
        sc_ln1, sc_ln2 = sb("sc_ln1", [P, KT, NB]), sb("sc_ln2", [P, KT, NB])
        sc_ada, sh_ada = sb("sc_ada", [P, KT, NB]), sb("sh_ada", [P, KT, NB])
        lnw = sb("lnw", [P, 2, KT])
        bada = sb("bada", [P, 2 * KT])
        idn = sb("idn", [P, P])
        condt = sb("condt", [P, KT, NB])
        rope1t = sb("rope1t", [P, 2, HD1])
        minus_half = sb("minus_half", [P, 1])
        stat = sb("stat", [P, 6, NT])

        ps = ctx.enter_context(nc.psum_tensor("ps", [P, 8, 512], F32))

        with ExitStack() as early:
            adaw = sb("adaw", [P, KT, 4 * D], into=early)
            wst = sb("wst", [P, KT, 2 * QK0], into=early)
            wost = sb("wost", [P, KT, D], into=early)
        mlp = ExitStack()
        h2h = sb("h2h", [P, KT, NTOK], F32R, mlp)
        h2l = sb("h2l", [P, KT, NTOK], F32R, mlp)
        mst = [sb("mst0", [P, 3, KT * P], into=mlp)]
        mwh, mwl = [sb("mwh0", [P, 3, KT * P], F32R, mlp)], [sb("mwl0", [P, 3, KT * P], F32R, mlp)]
        with ExitStack() as l0:
            cos0, sin0 = sb("cos0", [P, NT, HD0], into=l0), sb("sin0", [P, NT, HD0], into=l0)
            xn, xn2 = sb("xn", [P, D], into=l0), sb("xn2", [P, D], into=l0)
            sq, sq2 = sb("sq", [P, D], into=l0), sb("sq2", [P, D], into=l0)
            hf, gf = sb("hf", [P, KT, P], into=l0), sb("gf", [P, KT, P], into=l0)
            hh, hl = sb("hh", [P, KT, P], F32R, l0), sb("hl", [P, KT, P], F32R, l0)
            t1, t2 = sb("t1", [P, 2, 5, HD0], into=l0), sb("t2", [P, 2, 5, HD0], into=l0)
            qr = sb("qr", [P, 10 * HD0], into=l0)
            qT, kT = sb("qT", [P, KT, P], into=l0), sb("kT", [P, P], into=l0)
            ex = sb("ex", [P, KT, 2, S], into=l0)
            pT = sb("pT", [P, KT, P], into=l0)
            bdv = [sb(f"bdv{i}", [P, 2, 2 * HD0], into=l0) for i in range(2)]
            ch, cl = sb("ch", [P, KT, P], F32R, l0), sb("cl", [P, KT, P], F32R, l0)
            smx = sb("smx", [P, 3, 2 * KT], into=l0)
            posi, posf = sb("posi", [P, NT], I32, l0), sb("posf", [P, NT], into=l0)
            invt = sb("invt", [P, HD0 // 2], into=l0)
        mst.append(sb("mst1", [P, 3, KT * P], into=mlp))
        mwh.append(sb("mwh1", [P, 3, KT * P], F32R, mlp))
        mwl.append(sb("mwl1", [P, 3, KT * P], F32R, mlp))
        sg, af = sb("sg", [P, TB_TOKENS], into=mlp), sb("af", [P, TB_TOKENS], into=mlp)
        ah = [sb(f"ah{i}", [P, TB_TOKENS], F32R, mlp) for i in range(2)]
        al = [sb(f"al{i}", [P, TB_TOKENS], F32R, mlp) for i in range(2)]
        l1st = sb("l1st", [P, KT, 2 * QK1], into=mlp)
        mlp.close()
        yn, yf = sb("yn", [P, D]), sb("yf", [P, KT, P])
        ys = sb("ys", [P, KT, P])
        yh, yl = sb("yh", [P, KT, P], F32R), sb("yl", [P, KT, P], F32R)
        u1, u2 = sb("u1", [P, 2, 10, HD1]), sb("u2", [P, 2, 10, HD1])
        qr1 = sb("qr1", [P, D])
        lat, lath, latl = sb("lat", [P, P]), sb("lath", [P, P], F32R), sb("latl", [P, P], F32R)
        ku1, ku2, kr1 = sb("ku1", [P, KT, HD1]), sb("ku2", [P, KT, HD1]), sb("kr1", [P, KT, 4, HD1])
        qk1 = sb("qk1", [P, KT, 2, P])
        ex1 = sb("ex1", [P, KT, 4, S])
        pT1 = sb("pT1", [P, 2 * KT, P])
        bdv1 = [sb(f"bdv1_{i}", [P, 2, KT, 2 * HD1]) for i in range(2)]
        yc, ycl = sb("yc", [P, KT, P], F32R), sb("ycl", [P, KT, P], F32R)
        smx1 = sb("smx1", [P, 3, 4 * KT])
        bns = sb("bns", [P, 6])
        mv = [sb(f"mv{i}", [P, 2]) for i in range(2)]
        fin = [sb(f"fin{i}", [P, D]) for i in range(2)]

        (ld_cond, ld_ada, ld_x, ld_qkv, ld_wo, ld_small) = [sem("ld_" + n) for n in
                                                            "cond ada x qkv wo small".split()]
        ada_mm, ada_done, zeroed = sem("ada_mm"), sem("ada_done"), sem("zeroed")
        ang_step, ang_ready, rope_tab = sem("ang_step"), sem("ang_ready"), sem("rope_tab")
        w0h, w0l, w0ol = sem("w0h"), sem("w0l"), sem("w0ol")
        (a_ssq, a_ms, a_rstd, a_xn, a_xT, a_hf, a_hh, a_hl, a_qkv, a_rope, a_v, a_qr, a_qkT, a_qT, a_kT,
         a_sc, a_max, a_ds, a_ex, a_sum, a_rec, a_p, a_pTr, a_pT, a_ctx, a_ch, a_cl, a_wo, a_x,
         a_ssq2, a_ms2, a_rstd2, a_xn2, a_x2T, a_gf, a_h2h, a_h2l) = [sem("a_" + n) for n in (
            "ssq ms rstd xn xT hf hh hl qkv rope v qr qkT qT kT sc max ds ex sum rec p pTr pT ctx ch cl "
            "wo x ssq2 ms2 rstd2 xn2 x2T gf h2h h2l").split()]
        m_ld = [sem(f"m_ld{i}") for i in range(2)]
        (m_wh, m_wl, m_gate, m_up, m_sg, m_af, m_ah, m_al, m_down, m_x) = [sem("m_" + n) for n in (
            "wh wl gate up sg af ah al down x").split()]
        ld_l1, w1h, w1l = sem("ld_l1"), sem("w1h"), sem("w1l")
        (b_bn, b_mv, b_var, b_rstd, b_nb, b_xn, b_xT, b_ys, b_yf, b_hh, b_hl, b_qc, b_rope, b_lat, b_qr,
         b_latT, b_lath, b_latl, b_kv, b_krope, b_kr, b_v, b_qkT, b_qka, b_qkb, b_sc, b_max, b_ds, b_ex,
         b_sum, b_rec, b_p, b_pTr, b_pTa, b_pTb, b_ctx, b_ch, b_cl, b_wo, b_out, b_zero) = [
            sem("b_" + n) for n in (
            "bn mv var rstd nb xn xT ys yf hh hl qc rope lat qr latT lath latl kv krope kr v qkT qT kT sc "
            "max ds ex sum rec p pTr pTa pTb ctx ch cl wo out zero").split()]
        b_st = [sem(f"b_st{i}") for i in range(2)]

        def bank(k):
            return ps[:, k, :]

        def by_feature(ap):
            return ap.rearrange("p (k n) -> p k n", k=KT)

        def by_entry(ap):
            return ap.rearrange("p k (b s) -> p k b s", b=2)

        def scale_of(tab, t):
            return tab[:, :, bass.ds(t.n * 2, 2)].unsqueeze(3).broadcast_to([P, KT, 2, S])

        def heads(k, hd):
            return ps[:, 1:3, 0:320].rearrange("p c (h d) -> p c h d", d=hd)

        wcols = {0: (WqT, WkT, WvT), 1: (Wq1T, WkdT)}

        def load_qkv(eng, dst, layer, signal):
            at = 0
            for w in wcols[layer]:
                n = w.shape[1]
                eng.dma_start(dst[:, :, at:at + n], w.rearrange("(k p) n -> p k n", p=P)).then_inc(signal, 16)
                at += n

        block = ctx.enter_context(nc.Block())

        @block.sync
        def _(sp):
            xv = x.rearrange("(t p) d -> p t d", p=P)
            sp.dma_start(condt[:, :, :], condT.rearrange("(k p) b -> p k b", p=P)).then_inc(ld_cond, 16)
            for w, at in ((ln1_twT, 0), (ln2_twT, D), (adaT, 2 * D)):
                sp.dma_start(adaw[:, :, at:at + w.shape[1]],
                             w.rearrange("(k p) n -> p k n", p=P)).then_inc(ld_ada, 16)
            sp.dma_start(xres[:, :, :], xv).then_inc(ld_x, 16)
            load_qkv(sp, wst, 0, ld_qkv)
            sp.dma_start(wost[:, :, :], WoT.rearrange("(k p) n -> p k n", p=P)).then_inc(ld_wo, 16)

            def load_group(g, slot, reused):
                if reused:
                    wait(sp, m_wh, g - 1)
                    wait(sp, m_wl, g - 1)
                for n, w in enumerate((WgT, WuT)):
                    sp.dma_start(mst[slot][:, n, :].rearrange("p (k m) -> p k m", k=KT),
                                 w[:, bass.ds(g * P, P)].rearrange("(k p) m -> p k m", p=P)
                                 ).then_inc(m_ld[slot], 16)
                sp.dma_start(mst[slot][:, 2, :], WdT[bass.ds(g * P, P), :]).then_inc(m_ld[slot], 16)

            load_group(0, 0, False)
            wait(sp, a_h2l, NT)
            load_group(1, 1, False)
            load_qkv(sp, l1st, 1, ld_l1)
            with sp.Fori(1, NG // 2) as pair:
                for k in range(2):
                    load_group(pair * 2 + k, k, True)
            wait(sp, w1h, 1)
            wait(sp, w1l, 1)
            sp.dma_start(l1st[:, 0:KT, 0:D], Wo1T.rearrange("(k p) n -> p k n", p=P)).then_inc(ld_l1, 16)
            sp.dma_start(l1st[:, 0, D:D + P], WkuT).then_inc(ld_l1, 16)
            sp.dma_start(l1st[:, 1, D:D + P], WvuT).then_inc(ld_l1, 16)
            with sp.Fori(0, NT // 2) as pair:
                for k in range(2):
                    t = pair * 2 + k
                    sp.wait_ge(b_out, t + 1)
                    sp.dma_start(out[bass.ds(t * P, P), :], fin[k][:, :]).then_inc(b_st[k], 16)
            for k in range(2):
                sp.wait_ge(b_st[k], 16 * (NT // 2))

        @block.gpsimd
        def _(pool):
            for dst, srcs in ((idn[:, :], ident), (rope1t[:, :, :], rope1), (posi[:, :], pos),
                              (invt[:, :], invf), (bada[:, :], b_ada),
                              (lnw[:, 0, :], ln1_w),
                              (lnw[:, 1, :], ln2_w)):
                pool.dma_start(dst, srcs).then_inc(ld_small, 16)
            for i in range(2):
                pool.memset(bdv[i][:, :, :], 0.0).then_inc(zeroed, 1)
            pool.memset(minus_half[:, :], -0.5).then_inc(zeroed, 1)
            pool.wait_ge(zeroed, 3)
            pool.wait_ge(w0h, 2)
            pool.tensor_tensor(wol[:, :, :], wost[:, :, :], woh[:, :, :], ALU.subtract).then_inc(w0ol, 1)

            def inv_root(col, signal):
                pool.tensor_tensor(col, col, minus_half[:, :], ALU.pow).then_inc(signal, 1)

            def rstd(t):
                wait(pool, a_ms, t.n + 1)
                inv_root(stat[:, 1, bass.ds(t.n, 1)], a_rstd)

            def rstd2(t):
                wait(pool, a_ms2, t.n + 1)
                inv_root(stat[:, 3, bass.ds(t.n, 1)], a_rstd2)

            def low_h(t):
                wait(pool, a_hh, t.n + 1)
                wait(pool, a_qkv, t.n)
                pool.tensor_tensor(hl[:, :, :], hf[:, :, :], hh[:, :, :], ALU.subtract).then_inc(a_hl, 1)

            def rope_sum(t):
                wait(pool, a_rope, t.n + 1)
                wait(pool, a_qkT, t.n)
                u, v = (tile[:, :, :, :].rearrange("p c h d -> p (c h d)") for tile in (t1, t2))
                nk = D + HD0
                pool.tensor_tensor(qr[:, 0:nk], u[:, 0:nk], v[:, 0:nk], ALU.add)
                pool.tensor_tensor(qr[:, nk:nk + HD0], u[:, D:nk], v[:, D:nk], ALU.add).then_inc(a_qr, 1)

            def low_h2(t):
                wait(pool, a_h2h, t.n + 1)
                at = bass.ds(t.n * P, P)
                pool.tensor_tensor(h2l[:, :, at], gf[:, :, :], h2h[:, :, at], ALU.subtract).then_inc(a_h2l, 1)

            run_tiles(pool, NT, [(rstd, 2), (low_h2, -2), (rope_sum, 1), (rstd2, -1), (low_h, 2)])

            def split_group(g, slot):
                pool.wait_ge(m_wh, g + 1)
                pool.tensor_tensor(mwl[slot][:, :, :], mst[slot][:, :, :], mwh[slot][:, :, :],
                                   ALU.subtract).then_inc(m_wl, 1)

            split_group(0, 0)
            split_group(1, 1)
            with pool.Fori(1, NG // 4) as pair:
                for k in range(2):
                    split_group(pair * 2 + k, k)
            pool.wait_ge(w1h, 1)
            pool.tensor_tensor(wql[:, :, :], l1st[:, :, :], wqh[:, :, :], ALU.subtract).then_inc(w1l, 1)
            with pool.Fori(NG // 4, NG // 2) as pair:
                for k in range(2):
                    split_group(pair * 2 + k, k)
            pool.wait_ge(w1h, 3)
            pool.tensor_tensor(wol[:, :, :], l1st[:, :, 0:D], woh[:, :, :], ALU.subtract).then_inc(w1l, 1)
            pool.tensor_tensor(kvl[:, :].rearrange("p (c n) -> p c n", c=2), l1st[:, 0:2, D:D + P],
                               kvh[:, :].rearrange("p (c n) -> p c n", c=2), ALU.subtract).then_inc(w1l, 1)
            pool.wait_ge(m_x, NG * NT)
            pool.wait_ge(w1l, 3)
            for i in range(2):
                pool.memset(bdv1[i][:, :, :, :], 0.0).then_inc(b_zero, 1)

            def shift_h(t):
                wait(pool, b_ys, t.n + 1)
                wait(pool, b_hh, t.n)
                wait(pool, b_hl, t.n)
                pool.tensor_tensor(by_entry(yf[:, :, :]), by_entry(ys[:, :, :]), scale_of(sh_ada, t),
                                   ALU.add).then_inc(b_yf, 1)

            def rstd1(t):
                wait(pool, b_var, t.n + 1)
                inv_root(stat[:, 4, bass.ds(t.n, 1)], b_rstd)

            def low_y(t):
                wait(pool, b_hh, t.n + 1)
                wait(pool, b_qc, t.n)
                pool.tensor_tensor(yl[:, :, :], yf[:, :, :], yh[:, :, :], ALU.subtract).then_inc(b_hl, 1)

            def rope_sum1(t):
                wait(pool, b_rope, t.n + 1)
                wait(pool, b_qkT, t.n)
                pool.tensor_tensor(qr1[:, :], u1[:, :, :, :].rearrange("p c h d -> p (c h d)")[:, 0:D],
                                   u2[:, :, :, :].rearrange("p c h d -> p (c h d)")[:, 0:D],
                                   ALU.add).then_inc(b_qr, 1)

            def norm_p(t):
                wait(pool, b_rec, t.n + 1)
                pool.tensor_tensor(ex1[:, :, :, :].rearrange("p j g s -> p g j s"),
                                   ex1[:, :, :, :].rearrange("p j g s -> p g j s"),
                                   smx1[:, 2, :].rearrange("p (g j) -> p g j", g=4).unsqueeze(3)
                                   .broadcast_to([P, 4, KT, S]), ALU.mult).then_inc(b_p, 1)

            run_tiles(pool, NT, [(rstd1, 2), (norm_p, 0), (rope_sum1, 1), (shift_h, 2), (low_y, 2)])

        @block.tensor
        def _(pe):
            def three(dst, lh, ll, rh, rl, start, stop):
                pe.matmul(dst, lh, rh, start=start, stop=False)
                pe.matmul(dst, ll, rh, start=False, stop=False)
                return pe.matmul(dst, lh, rl, start=False, stop=stop)

            pe.wait_ge(ld_cond, 16)
            pe.wait_ge(ld_ada, 48)
            for m in range(4 * KT):
                for k in range(KT):
                    mm = pe.matmul(ps[:, 0, NB * m:NB * (m + 1)], adaw[:, k, P * m:P * (m + 1)],
                                   condt[:, k, :], start=(k == 0), stop=(k == KT - 1))
            mm.then_inc(ada_mm, 1)
            pe.wait_ge(ld_small, 112)

            def x_T(t):
                wait(pe, a_xn, t.n + 1)
                if isinstance(t.n, int) and t.n < 3:
                    pe.wait_ge(ada_done, 4)
                wait(pe, a_hf, t.n)
                wait(pe, a_gf, t.n - 3)
                for k in range(KT):
                    mm = pe.transpose(ps[:, 0, P * k:P * (k + 1)], xn[:, P * k:P * (k + 1)], idn[:, :])
                mm.then_inc(a_xT, 1)

            def qkv(t):
                if isinstance(t.n, int) and t.n == 0:
                    pe.wait_ge(w0h, 1)
                    pe.wait_ge(w0l, 1)
                wait(pe, a_hh, t.n + 1)
                wait(pe, a_hl, t.n + 1)
                wait(pe, a_rope, t.n)
                wait(pe, a_v, t.n)
                for c in range(2):
                    cols = slice(QK0 * c, QK0 * (c + 1))
                    for k in range(KT):
                        mm = three(ps[:, 1 + c, 0:QK0], hh[:, k, :], hl[:, k, :], wqh[:, k, cols],
                                   wql[:, k, cols], k == 0, k == KT - 1)
                mm.then_inc(a_qkv, 1)

            def qk_T(t):
                wait(pe, a_qr, t.n + 1)
                wait(pe, a_pT, t.n)
                wait(pe, a_ds, t.n)
                for k in range(KT):
                    pe.transpose(ps[:, 5, P * k:P * (k + 1)], qr[:, P * k:P * (k + 1)], idn[:, :])
                mm = pe.transpose(ps[:, 3, 256:384], qr[:, D:D + 2 * HD0], idn[:, :])
                mm.then_inc(a_qkT, 1)

            def scores_free(t):
                wait(pe, a_qT, t.n + 1)
                wait(pe, a_kT, t.n + 1)

            def scores(t):
                for j in range(KT):
                    for b in range(2):
                        for i in range(2):
                            r, q = slice(HD0 * i, HD0 * (i + 1)), slice(S * b, S * (b + 1))
                            mm = pe.matmul(ps[q, 3 + i, S * j:S * (j + 1)], qT[r, j, q], kT[r, q],
                                           start=True, stop=True)
                mm.then_inc(a_sc, 1)

            def p_T(t):
                wait(pe, a_p, t.n + 1)
                wait(pe, a_qT, t.n + 1)
                for j in range(KT):
                    mm = pe.transpose(ps[:, 5, P * j:P * (j + 1)],
                                      ex[:, j, :, :].rearrange("p i s -> p (i s)"), idn[:, :])
                mm.then_inc(a_pTr, 1)

            def context(t):
                wait(pe, a_pT, t.n + 1)
                wait(pe, a_v, t.n + 1)
                wait(pe, a_ch, t.n)
                wait(pe, a_cl, t.n)
                for b in range(2):
                    mm = pe.matmul(ps[:, 6, 256 * b:256 * (b + 1)], bdv[t.par][:, b, :],
                                   pT[:, :, S * b:S * (b + 1)], start=True, stop=True)
                mm.then_inc(a_ctx, 1)

            def project(t):
                if isinstance(t.n, int) and t.n == 0:
                    pe.wait_ge(w0ol, 1)
                wait(pe, a_ch, t.n + 1)
                wait(pe, a_cl, t.n + 1)
                wait(pe, a_x, t.n)
                for k in range(KT):
                    mm = three(bank(7), ch[:, k, :], cl[:, k, :], woh[:, k, :], wol[:, k, :],
                               k == 0, k == KT - 1)
                mm.then_inc(a_wo, 1)

            def x2_T(t):
                wait(pe, a_xn2, t.n + 1)
                wait(pe, a_gf, t.n)
                wait(pe, a_hf, min(t.n + 4, NT) if isinstance(t.n, int) else t.n + 4)
                for k in range(KT):
                    mm = pe.transpose(ps[:, 0, P * k:P * (k + 1)], xn2[:, P * k:P * (k + 1)], idn[:, :])
                mm.then_inc(a_x2T, 1)

            run_tiles(pe, NT, [(scores_free, 0), (x2_T, -2), (scores, 0), (qkv, 1), (project, -1), (p_T, 0), (x_T, 2),
                               (qk_T, 1), (context, 0)])

            def gate_up(g, r, slot, first):
                n = g * NBLK + r
                if r == 0:
                    pe.wait_ge(m_wl, g + 1)
                if first:
                    pe.wait_ge(a_h2l, NT)
                    pe.wait_ge(a_h2h, NT)
                wait(pe, m_sg, n - 1)
                wait(pe, m_af, n - 1)
                tok = slice(TB_TOKENS * r, TB_TOKENS * (r + 1))
                for w, done in ((0, m_gate), (1, m_up)):
                    for k in range(KT):
                        f = slice(P * k, P * (k + 1))
                        mm = three(bank(2 * w + r % 2), mwh[slot][:, w, f], mwl[slot][:, w, f],
                                   h2h[:, k, tok], h2l[:, k, tok], k == 0, k == KT - 1)
                    mm.then_inc(done, 1)

            def down(n, act, slot):
                pe.wait_ge(m_al, n + 1)
                for i in range(TPB):
                    wait(pe, m_x, (n - 1) * TPB + i + 1)
                    f = slice(P * i, P * (i + 1))
                    three(bank(4 + i), ah[act][:, f], al[act][:, f], mwh[slot][:, 2, :],
                          mwl[slot][:, 2, :], True, True).then_inc(m_down, 1)

            def group(g, slot, first=False):
                for r in range(NBLK):
                    gate_up(g, r, slot, first and r == 0)
                    if not (first and r == 0):
                        down(g * NBLK + (r - 1), (r - 1) % 2, slot if r else 1 - slot)

            group(0, 0, True)
            with pe.Fori(0, NG // 2 - 1) as pair:
                group(pair * 2 + 1, 1)
                group(pair * 2 + 2, 0)
            group(NG - 1, 1)
            down(NG * NBLK - 1, 1, 1)

            pe.wait_ge(w1l, 3)
            pe.wait_ge(m_x, NG * NT)

            def y_T(t):
                wait(pe, b_xn, t.n + 1)
                wait(pe, b_ys, t.n)
                for k in range(KT):
                    mm = pe.transpose(ps[:, 0, P * k:P * (k + 1)], yn[:, P * k:P * (k + 1)], idn[:, :])
                mm.then_inc(b_xT, 1)

            def q_latent(t):
                wait(pe, b_hl, t.n + 1)
                wait(pe, b_rope, t.n)
                wait(pe, b_krope, t.n)
                wait(pe, b_v, t.n)
                for c in range(2):
                    cols = slice(QK1 * c, QK1 * (c + 1))
                    for k in range(KT):
                        mm = three(ps[:, 1 + c, 0:QK1], yh[:, k, :], yl[:, k, :], wqh[:, k, cols],
                                   wql[:, k, cols], k == 0, k == KT - 1)
                mm.then_inc(b_qc, 1)

            def latent_T(t):
                wait(pe, b_lat, t.n + 1)
                wait(pe, b_ds, t.n)
                pe.transpose(ps[:, 3, 256:384], lat[:, :], idn[:, :]).then_inc(b_latT, 1)

            def keys_values(t):
                wait(pe, b_latl, t.n + 1)
                wait(pe, b_rope, t.n + 1)
                for c in range(2):
                    cols = slice(P * c, P * (c + 1))
                    mm = three(ps[:, 1 + c, QK1:QK1 + P], lath[:, :], latl[:, :], kvh[:, cols],
                               kvl[:, cols], True, True)
                mm.then_inc(b_kv, 1)

            def qk_T1(t):
                wait(pe, b_qr, t.n + 1)
                wait(pe, b_kr, t.n + 1)
                wait(pe, b_pTa, t.n)
                wait(pe, b_pTb, t.n)
                for j in range(KT):
                    pe.transpose(ps[:, 3 + j, 256:384], qr1[:, P * j:P * (j + 1)], idn[:, :])
                    mm = pe.transpose(ps[:, 3 + j, 384:512],
                                      kr1[:, j, :, :].rearrange("p g d -> p (g d)"), idn[:, :])
                mm.then_inc(b_qkT, 1)

            def scores1(t):
                wait(pe, b_qka, t.n + 1)
                wait(pe, b_qkb, t.n + 1)
                for j in range(KT):
                    for b in range(2):
                        for g in range(4):
                            r, q = slice(HD1 * g, HD1 * (g + 1)), slice(S * b, S * (b + 1))
                            mm = pe.matmul(ps[q, 3 + g, S * j:S * (j + 1)], qk1[r, j, 0, q], qk1[r, j, 1, q],
                                           start=True, stop=True, tile_position=(HD1 * g, S * b))
                mm.then_inc(b_sc, 1)

            def p_T1(t):
                wait(pe, b_p, t.n + 1)
                wait(pe, b_lath, t.n + 2 if not isinstance(t.n, int) else min(t.n + 2, NT))
                wait(pe, b_latl, t.n + 2 if not isinstance(t.n, int) else min(t.n + 2, NT))
                for j in range(KT):
                    for i in range(2):
                        mm = pe.transpose(ps[:, 3 + j, 256 + P * i:256 + P * (i + 1)],
                                          ex1[:, j, 2 * i:2 * i + 2, :].rearrange("p g s -> p (g s)"), idn[:, :])
                mm.then_inc(b_pTr, 1)

            def context1(t):
                wait(pe, b_pTa, t.n + 1)
                wait(pe, b_pTb, t.n + 1)
                wait(pe, b_v, t.n + 1)
                wait(pe, b_out, t.n)
                for j in range(KT):
                    for b in range(2):
                        for i in range(2):
                            mm = pe.matmul(ps[S * i:S * (i + 1), 7, P * j + S * b:P * j + S * (b + 1)],
                                           bdv1[t.par][:, b, j, :], pT1[:, 2 * j + i, S * b:S * (b + 1)],
                                           start=True, stop=True)
                mm.then_inc(b_ctx, 1)

            def project1(t):
                wait(pe, b_ch, t.n + 1)
                wait(pe, b_cl, t.n + 1)
                for k in range(KT):
                    mm = three(bank(7), yc[:, k, :], ycl[:, k, :], woh[:, k, :], wol[:, k, :],
                               k == 0, k == KT - 1)
                mm.then_inc(b_wo, 1)

            run_tiles(pe, NT, [(scores1, 0), (q_latent, 1), (project1, -1), (latent_T, 1), (p_T1, 0),
                               (keys_values, 1), (context1, 0), (qk_T1, 1), (y_T, 2)])

        @block.vector
        def _(dve):
            dve.wait_ge(ld_small, 112)
            dve.tensor_copy(posf[:, :], posi[:, :]).then_inc(ang_step, 1)
            NA = HD0 // 2
            flat = lambda tile: tile[:, :, :, :].rearrange("p c h d -> p (c h d)")[:, 0:NT * NA]
            angle, turns, red = flat(t1), flat(t2), flat(ex)
            dve.wait_ge(ang_step, 1)
            dve.tensor_tensor(angle.rearrange("p (t a) -> p t a", t=NT),
                              posf[:, :].unsqueeze(2).broadcast_to([P, NT, NA]),
                              invt[:, :].unsqueeze(1).broadcast_to([P, NT, NA]), ALU.mult).then_inc(ang_step, 1)
            dve.wait_ge(ang_step, 2)
            dve.tensor_scalar(turns, angle, 1.0 / TWO_PI, ROUND, ALU.mult, ALU.add).then_inc(ang_step, 1)
            dve.wait_ge(ang_step, 3)
            dve.tensor_scalar(turns, turns, -ROUND, None, ALU.add).then_inc(ang_step, 1)
            step = 4
            src = angle
            for part in (C1, C2, C3):
                dve.wait_ge(ang_step, step)
                dve.scalar_tensor_tensor(out=red, in0=turns, scalar=-part, in1=src, op0=ALU.mult,
                                         op1=ALU.add).then_inc(ang_step, 1)
                src = red
                step += 1
            dve.wait_ge(ang_step, step)
            dve.tensor_scalar(red, red, float(np.float32(3.1415925)), -float(np.float32(3.1415925)),
                              ALU.min, ALU.max).then_inc(ang_step, 1)
            dve.wait_ge(ang_step, step + 1)
            dve.scalar_tensor_tensor(out=angle, in0=red, scalar=-1.0, in1=red, op0=ALU.mult,
                                     op1=ALU.max).then_inc(ang_step, 1)
            dve.wait_ge(ang_step, step + 2)
            dve.tensor_scalar(angle, angle, -1.0, float(np.pi / 2), ALU.mult, ALU.add).then_inc(ang_ready, 1)

            dve.wait_ge(ada_mm, 1)
            adap = lambda m: ps[:, 0, NB * m:NB * (m + 1)]
            for n, tab in enumerate((sc_ln1, sc_ln2)):
                for k in range(KT):
                    ins = dve.tensor_scalar(tab[:, k, :], adap(KT * n + k), 1.0, lnw[:, n, k:k + 1],
                                            ALU.add, ALU.mult)
                ins.then_inc(ada_done, 1)
            for k in range(KT):
                ins = dve.tensor_scalar(sc_ada[:, k, :], adap(2 * KT + k), bada[:, k:k + 1], 1.0,
                                        ALU.add, ALU.add)
            ins.then_inc(ada_done, 1)
            for k in range(KT):
                ins = dve.tensor_scalar(sh_ada[:, k, :], adap(3 * KT + k), bada[:, KT + k:KT + k + 1], None,
                                        ALU.add)
            ins.then_inc(ada_done, 1)
            dve.wait_ge(w0h, 1)
            dve.wait_ge(ada_done, 4)
            dve.tensor_tensor(wql[:, :, :], wst[:, :, :], wqh[:, :, :], ALU.subtract).then_inc(w0l, 1)
            dve.wait_ge(rope_tab, 4)

            def mean_sq(t):
                wait(dve, a_ssq, t.n + 1)
                dve.tensor_scalar(stat[:, 1, bass.ds(t.n, 1)], stat[:, 0, bass.ds(t.n, 1)], 1e-6, None,
                                  ALU.add).then_inc(a_ms, 1)

            def mean_sq2(t):
                wait(dve, a_ssq2, t.n + 1)
                dve.tensor_scalar(stat[:, 3, bass.ds(t.n, 1)], stat[:, 2, bass.ds(t.n, 1)], 1e-6, None,
                                  ALU.add).then_inc(a_ms2, 1)

            def scale_h(t):
                wait(dve, a_xT, t.n + 1)
                wait(dve, a_hl, t.n)
                dve.tensor_tensor(by_entry(hf[:, :, :]), by_entry(by_feature(bank(0))), scale_of(sc_ln1, t),
                                  ALU.mult).then_inc(a_hf, 1)

            def scale_h2(t):
                wait(dve, a_x2T, t.n + 1)
                wait(dve, a_h2l, t.n)
                dve.tensor_tensor(by_entry(gf[:, :, :]), by_entry(by_feature(bank(0))), scale_of(sc_ln2, t),
                                  ALU.mult).then_inc(a_gf, 1)

            def rope_mul(t):
                wait(dve, a_qkv, t.n + 1)
                wait(dve, a_qr, t.n)
                q, half = heads(0, HD0), HD0 // 2
                tab = lambda m, a, b: (m[:, bass.ds(t.n, 1), a:b].unsqueeze(1)
                                       .broadcast_to([P, 2, 5, b - a]))
                dve.tensor_tensor(t1[:, :, :, :], q, tab(cos0, 0, HD0), ALU.mult)
                dve.tensor_tensor(t2[:, :, :, 0:half], q[:, :, :, half:HD0], tab(sin0, 0, half), ALU.mult)
                dve.tensor_tensor(t2[:, :, :, half:HD0], q[:, :, :, 0:half], tab(sin0, half, HD0),
                                  ALU.mult).then_inc(a_rope, 1)

            def keys(t):
                wait(dve, a_qkT, t.n + 1)
                wait(dve, a_sc, t.n)
                dve.tensor_copy(kT[:, :], ps[:, 3, 256:384]).then_inc(a_kT, 1)

            def sc_view():
                return ps[:, 3:5, 0:256].rearrange("p i (j s) -> p i j s", j=KT)

            def ex_view():
                return ex[:, :, :, :].rearrange("p j i s -> p i j s")

            def row(n):
                return (smx[:, n, :].rearrange("p (i j) -> p i j", i=2).unsqueeze(3)
                        .broadcast_to([P, 2, KT, S]))

            def softmax_sub(t):
                wait(dve, a_sc, t.n + 1)
                wait(dve, a_pTr, t.n)
                dve.tensor_reduce(smx[:, 0, :].rearrange("p (i j) -> p i j", i=2), sc_view(), AX_X,
                                  ALU.max).then_inc(a_max, 1)
                wait(dve, a_max, t.n + 1)
                dve.tensor_tensor(ex_view(), sc_view(), row(0), ALU.subtract).then_inc(a_ds, 1)

            def softmax_norm(t):
                wait(dve, a_ex, t.n + 1)
                dve.tensor_reduce(smx[:, 1, :].rearrange("p (i j) -> p i j", i=2), ex_view(), AX_X,
                                  ALU.add).then_inc(a_sum, 1)
                wait(dve, a_sum, t.n + 1)
                dve.reciprocal(smx[:, 2, :], smx[:, 1, :]).then_inc(a_rec, 1)
                wait(dve, a_rec, t.n + 1)
                dve.tensor_tensor(ex_view(), ex_view(), row(2), ALU.mult).then_inc(a_p, 1)

            def low_ctx(t):
                wait(dve, a_ch, t.n + 1)
                wait(dve, a_wo, t.n)
                dve.tensor_tensor(by_entry(cl[:, :, :]), bank(6).rearrange("p (b j s) -> p j b s", b=2, j=KT),
                                  by_entry(ch[:, :, :]), ALU.subtract).then_inc(a_cl, 1)

            def add_x(t):
                wait(dve, a_wo, t.n + 1)
                at = xres[:, bass.ds(t.n, 1), :].rearrange("p o d -> p (o d)")
                dve.tensor_tensor(at, bank(7), at, ALU.add).then_inc(a_x, 1)

            run_tiles(dve, NT, [(mean_sq, 2), (softmax_sub, 0), (scale_h2, -2), (softmax_norm, 0),
                                (rope_mul, 1), (add_x, -1), (scale_h, 2), (keys, 1), (mean_sq2, -1),
                                (low_ctx, 0)])

            def mlp_step(g, r):
                n = g * NBLK + r
                dve.wait_ge(m_sg, n + 1)
                dve.wait_ge(m_up, n + 1)
                wait(dve, m_al, n)
                wait(dve, m_ah, n)
                dve.tensor_tensor(af[:, :], bank(2 + r % 2), sg[:, :], ALU.mult).then_inc(m_af, 1)
                dve.wait_ge(m_ah, n + 1)
                wait(dve, m_down, TPB * (n - 1))
                dve.tensor_tensor(al[r % 2][:, :], af[:, :], ah[r % 2][:, :], ALU.subtract).then_inc(m_al, 1)

            def add_block(g, r):
                for i in range(TPB):
                    dve.wait_ge(m_down, (g * NBLK + r) * TPB + i + 1)
                    at = xres[:, TPB * (r % NBLK) + i, :]
                    dve.tensor_tensor(at, bank(4 + i), at, ALU.add).then_inc(m_x, 1)

            def mlp_group(g, first=False):
                for r in range(NBLK):
                    mlp_step(g, r)
                    if not (first and r == 0):
                        add_block(g, r - 1)

            mlp_group(0, True)
            with dve.Fori(1, NG) as g:
                mlp_group(g)
            add_block(NG - 1, NBLK - 1)
            dve.wait_ge(w1l, 3)
            dve.wait_ge(m_x, NG * NT)

            def stats1(t):
                wait(dve, b_xn, t.n)
                at = lambda n: stat[:, n, bass.ds(t.n, 1)]
                m = mv[t.par]
                dve.bn_stats(bns[:, :], xres[:, bass.ds(t.n, 1), :].rearrange("p o d -> p (o d)")
                             ).then_inc(b_bn, 1)

            def stats1_there(t):
                wait(dve, b_bn, t.n + 1)

            def mean_var(t):
                m, at = mv[t.par], lambda n: stat[:, n, bass.ds(t.n, 1)]
                dve.bn_aggr(m[:, :], bns[:, :]).then_inc(b_mv, 1)
                wait(dve, b_mv, t.n + 1)
                dve.tensor_scalar(at(4), m[:, 1:2], 1e-5, None, ALU.add).then_inc(b_var, 1)

            def mean_rstd(t):
                m, at = mv[t.par], lambda n: stat[:, n, bass.ds(t.n, 1)]
                wait(dve, b_rstd, t.n + 1)
                dve.scalar_tensor_tensor(out=at(5), in0=m[:, 0:1], scalar=-1.0, in1=at(4), op0=ALU.mult,
                                         op1=ALU.mult).then_inc(b_nb, 1)

            def scale_y(t):
                wait(dve, b_xT, t.n + 1)
                wait(dve, b_yf, t.n)
                dve.tensor_tensor(by_entry(ys[:, :, :]), by_entry(by_feature(bank(0))), scale_of(sc_ada, t),
                                  ALU.mult).then_inc(b_ys, 1)

            half1 = HD1 // 2

            def tab1(m, a, b, n):
                return rope1t[:, m, a:b].unsqueeze(1).unsqueeze(1).broadcast_to([P, n[0], n[1], b - a])

            def rope_mul1(t):
                wait(dve, b_lat, t.n + 1)
                wait(dve, b_qr, t.n)
                q = heads(0, HD1)
                dve.tensor_tensor(u1[:, :, :, :], q, tab1(0, 0, HD1, (2, 10)), ALU.mult)
                dve.tensor_tensor(u2[:, :, :, 0:half1], q[:, :, :, half1:HD1], tab1(1, 0, half1, (2, 10)),
                                  ALU.mult)
                dve.tensor_tensor(u2[:, :, :, half1:HD1], q[:, :, :, 0:half1], tab1(1, half1, HD1, (2, 10)),
                                  ALU.mult).then_inc(b_rope, 1)

            def low_latent(t):
                wait(dve, b_lath, t.n + 1)
                wait(dve, b_kv, t.n)
                dve.tensor_tensor(latl[:, :], ps[:, 3, 256:384], lath[:, :], ALU.subtract).then_inc(b_latl, 1)

            def key_rope(t):
                wait(dve, b_kv, t.n + 1)
                wait(dve, b_kr, t.n)
                wait(dve, b_qkT, t.n)
                k = ps[:, 1, QK1:QK1 + P].rearrange("p (j d) -> p j d", j=KT)
                tab = lambda m, a, b: rope1t[:, m, a:b].unsqueeze(1).broadcast_to([P, KT, b - a])
                dve.tensor_tensor(ku1[:, :, :], k, tab(0, 0, HD1), ALU.mult)
                dve.tensor_tensor(ku2[:, :, 0:half1], k[:, :, half1:HD1], tab(1, 0, half1), ALU.mult)
                dve.tensor_tensor(ku2[:, :, half1:HD1], k[:, :, 0:half1], tab(1, half1, HD1),
                                  ALU.mult).then_inc(b_krope, 1)
                wait(dve, b_krope, t.n + 1)
                rep = lambda tile: tile[:, :, :].unsqueeze(2).broadcast_to([P, KT, 4, HD1])
                dve.tensor_tensor(kr1[:, :, :, :], rep(ku1), rep(ku2), ALU.add).then_inc(b_kr, 1)

            def sc_view1():
                return ps[:, 3:7, 0:256].rearrange("p g (j s) -> p g j s", j=KT)

            def ex_view1():
                return ex1[:, :, :, :].rearrange("p j g s -> p g j s")

            def max_view1(n):
                return smx1[:, n, :].rearrange("p (g j) -> p g j", g=4)

            def softmax_sub1(t):
                wait(dve, b_sc, t.n + 1)
                wait(dve, b_pTr, t.n)
                dve.tensor_reduce(max_view1(0), sc_view1(), AX_X, ALU.max).then_inc(b_max, 1)
                wait(dve, b_max, t.n + 1)
                dve.tensor_tensor(ex_view1(), sc_view1(), max_view1(0).unsqueeze(3)
                                  .broadcast_to([P, 4, KT, S]), ALU.subtract).then_inc(b_ds, 1)

            def softmax_sum1(t):
                wait(dve, b_ex, t.n + 1)
                wait(dve, b_p, t.n)
                dve.tensor_reduce(max_view1(1), ex_view1(), AX_X, ALU.add).then_inc(b_sum, 1)
                wait(dve, b_sum, t.n + 1)
                dve.reciprocal(smx1[:, 2, :], smx1[:, 1, :]).then_inc(b_rec, 1)

            def queries_keys1(t):
                wait(dve, b_qkT, t.n + 1)
                wait(dve, b_sc, t.n)
                dve.tensor_copy(qk1[:, 2:4, :, :], ps[:, 5:7, 256:512].rearrange("p j (c n) -> p j c n", c=2)
                                ).then_inc(b_qkb, 1)

            def probs_T1(t):
                wait(dve, b_pTr, t.n + 1)
                wait(dve, b_ctx, t.n)
                dve.tensor_copy(pT1[:, KT:2 * KT, :].rearrange("p (j i) n -> p j i n", i=2),
                                ps[:, 5:7, 256:512].rearrange("p j (i n) -> p j i n", i=2)).then_inc(b_pTb, 1)

            def low_ctx1(t):
                wait(dve, b_ch, t.n + 1)
                wait(dve, b_wo, t.n)
                dve.tensor_tensor(ycl[:, :, :], by_feature(bank(7)), yc[:, :, :], ALU.subtract).then_inc(b_cl, 1)

            def add_out(t):
                wait(dve, b_wo, t.n + 1)
                wait(dve, b_st[t.par], (t.n - t.par) * 8)
                dve.tensor_tensor(fin[t.par][:, :], bank(7), xres[:, bass.ds(t.n, 1), :].rearrange(
                    "p o d -> p (o d)"), ALU.add).then_inc(b_out, 1)

            run_tiles(dve, NT, [(softmax_sub1, 0), (stats1, 2), (stats1_there, 2), (softmax_sum1, 0), (mean_var, 2), (rope_mul1, 1), (mean_rstd, 2),
                                (add_out, -1), (low_latent, 1), (probs_T1, 0), (key_rope, 1),
                                (queries_keys1, 1), (low_ctx1, 0), (scale_y, 2)])

        @block.scalar
        def _(act):
            NA = HD0 // 2
            flat = lambda tile: (tile[:, :, :, :].rearrange("p c h d -> p (c h d)")[:, 0:NT * NA]
                                 .rearrange("p (t a) -> p t a", t=NT))
            act.wait_ge(ang_ready, 1)
            act.activation(sin0[:, :, 0:NA], flat(ex), ACT.Sin, scale=-1.0).then_inc(rope_tab, 1)
            act.activation(sin0[:, :, NA:HD0], flat(ex), ACT.Sin).then_inc(rope_tab, 1)
            act.activation(cos0[:, :, 0:NA], flat(t1), ACT.Sin).then_inc(rope_tab, 1)
            act.activation(cos0[:, :, NA:HD0], flat(t1), ACT.Sin).then_inc(rope_tab, 1)
            act.wait_ge(ld_qkv, 48)
            act.copy(wqh[:, :, :], wst[:, :, :]).then_inc(w0h, 1)
            act.wait_ge(ld_wo, 16)
            act.copy(woh[:, :, :], wost[:, :, :]).then_inc(w0h, 1)
            act.wait_ge(ld_x, 16)
            act.wait_ge(zeroed, 2)

            def xt(t):
                return xres[:, bass.ds(t.n, 1), :].rearrange("p o d -> p (o d)")

            def square(t):
                wait(act, a_ssq, t.n)
                act.activation(sq[:, :], xt(t), ACT.Square, scale=float(D) ** -0.5,
                               accum_out=stat[:, 0, bass.ds(t.n, 1)]).then_inc(a_ssq, 1)

            def norm(t):
                wait(act, a_rstd, t.n + 1)
                wait(act, a_xT, t.n)
                act.activation(xn[:, :], xt(t), ACT.Copy, scale=stat[:, 1, bass.ds(t.n, 1)]).then_inc(a_xn, 1)

            def high_h(t):
                wait(act, a_hf, t.n + 1)
                wait(act, a_qkv, t.n)
                act.copy(hh[:, :, :], hf[:, :, :]).then_inc(a_hh, 1)

            def values(t):
                wait(act, a_rope, t.n + 1)
                wait(act, a_ctx, t.n - 1)
                for b in range(2):
                    for i in range(2):
                        ins = act.copy(bdv[t.par][HD0 * i:HD0 * (i + 1), b, HD0 * i:HD0 * (i + 1)],
                                       ps[S * b:S * (b + 1), 2, QK0 - HD0:QK0])
                ins.then_inc(a_v, 1)

            def queries(t):
                wait(act, a_qkT, t.n + 1)
                wait(act, a_sc, t.n)
                act.copy(qT[:, :, :], by_feature(bank(5))).then_inc(a_qT, 1)

            def softmax_exp(t):
                wait(act, a_ds, t.n + 1)
                act.activation(ex[:, :, :, :], ex[:, :, :, :], ACT.Exp, scale=float(HD0) ** -0.5
                               ).then_inc(a_ex, 1)

            def probs_T(t):
                wait(act, a_pTr, t.n + 1)
                wait(act, a_ctx, t.n)
                act.copy(pT[:, :, :], by_feature(bank(5))).then_inc(a_pT, 1)

            def high_ctx(t):
                wait(act, a_ctx, t.n + 1)
                wait(act, a_wo, t.n)
                act.copy(by_entry(ch[:, :, :]), bank(6).rearrange("p (b j s) -> p j b s", b=2, j=KT)
                         ).then_inc(a_ch, 1)

            def square2(t):
                wait(act, a_x, t.n + 1)
                wait(act, a_ssq2, t.n)
                act.activation(sq2[:, :], xt(t), ACT.Square, scale=float(D) ** -0.5,
                               accum_out=stat[:, 2, bass.ds(t.n, 1)]).then_inc(a_ssq2, 1)

            def norm2(t):
                wait(act, a_rstd2, t.n + 1)
                wait(act, a_x2T, t.n)
                act.activation(xn2[:, :], xt(t), ACT.Copy, scale=stat[:, 3, bass.ds(t.n, 1)]).then_inc(a_xn2, 1)

            def high_h2(t):
                wait(act, a_gf, t.n + 1)
                act.copy(h2h[:, :, bass.ds(t.n * P, P)], gf[:, :, :]).then_inc(a_h2h, 1)

            run_tiles(act, NT, [(square, 2), (softmax_exp, 0), (norm, 2), (high_h2, -2), (values, 1),
                                (probs_T, 0), (square2, -1), (queries, 1), (high_h, 2), (norm2, -1),
                                (high_ctx, 0)])

            def split_group(g, slot, reused):
                act.wait_ge(m_ld[slot], 48 * (1 + (g // 2 if isinstance(g, int) else 0)) if isinstance(g, int)
                            else (g - slot) * 24 + 48)
                if reused:
                    wait(act, m_down, (g - 1) * NBLK * TPB)
                act.copy(mwh[slot][:, :, :], mst[slot][:, :, :]).then_inc(m_wh, 1)

            def mlp_step(g, r):
                n = g * NBLK + r
                act.wait_ge(m_gate, n + 1)
                wait(act, m_af, n)
                act.activation(sg[:, :], bank(r % 2), ACT.Silu).then_inc(m_sg, 1)
                act.wait_ge(m_af, n + 1)
                wait(act, m_down, TPB * (n - 1))
                wait(act, m_al, n - 1)
                act.copy(ah[r % 2][:, :], af[:, :]).then_inc(m_ah, 1)

            def mlp_group(g, slot, nxt=True):
                for r in range(NBLK):
                    mlp_step(g, r)
                    if r == 1 and nxt:
                        split_group(g + 1, 1 - slot, not (isinstance(g, int) and g == 0))

            split_group(0, 0, False)
            act.wait_ge(a_h2l, NT)
            mlp_group(0, 0)
            mlp_group(1, 1)
            with act.Fori(1, NG // 4) as pair:
                for k in range(2):
                    mlp_group(pair * 2 + k, k)
            act.wait_ge(ld_l1, 32)
            act.copy(wqh[:, :, :], l1st[:, :, :]).then_inc(w1h, 1)
            with act.Fori(NG // 4, NG // 2 - 1) as pair:
                for k in range(2):
                    mlp_group(pair * 2 + k, k)
            mlp_group(NG - 2, 0)
            mlp_group(NG - 1, 1, False)
            act.wait_ge(ld_l1, 80)
            act.copy(woh[:, :, :], l1st[:, :, 0:D]).then_inc(w1h, 1)
            act.copy(kvh[:, :].rearrange("p (c n) -> p c n", c=2), l1st[:, 0:2, D:D + P]).then_inc(w1h, 1)
            act.wait_ge(w1l, 3)
            act.wait_ge(m_x, NG * NT)
            act.wait_ge(b_zero, 2)

            def norm1(t):
                wait(act, b_nb, t.n + 1)
                wait(act, b_xT, t.n)
                act.activation(yn[:, :], xt(t), ACT.Identity, bias=stat[:, 5, bass.ds(t.n, 1)],
                               scale=stat[:, 4, bass.ds(t.n, 1)]).then_inc(b_xn, 1)

            def high_y(t):
                wait(act, b_yf, t.n + 1)
                wait(act, b_qc, t.n)
                act.copy(yh[:, :, :], yf[:, :, :]).then_inc(b_hh, 1)

            def latent(t):
                wait(act, b_qc, t.n + 1)
                wait(act, b_latT, t.n)
                act.copy(lat[:, :], ps[:, 2, QK1 - P:QK1]).then_inc(b_lat, 1)

            def high_latent(t):
                wait(act, b_latT, t.n + 1)
                wait(act, b_kv, t.n)
                act.copy(lath[:, :], ps[:, 3, 256:384]).then_inc(b_lath, 1)

            def values1(t):
                wait(act, b_kv, t.n + 1)
                wait(act, b_ctx, t.n - 1)
                for b in range(2):
                    for i in range(2):
                        ins = act.copy(bdv1[t.par][S * i:S * (i + 1), b, :, HD1 * i:HD1 * (i + 1)],
                                       ps[S * b:S * (b + 1), 2, QK1:QK1 + P].rearrange("p (j d) -> p j d", j=KT))
                ins.then_inc(b_v, 1)

            def queries_keys1(t):
                wait(act, b_qkT, t.n + 1)
                wait(act, b_sc, t.n)
                act.copy(qk1[:, 0:2, :, :], ps[:, 3:5, 256:512].rearrange("p j (c n) -> p j c n", c=2)
                         ).then_inc(b_qka, 1)

            def softmax_exp1(t):
                wait(act, b_ds, t.n + 1)
                act.activation(ex1[:, :, :, :], ex1[:, :, :, :], ACT.Exp, scale=float(HD1) ** -0.5
                               ).then_inc(b_ex, 1)

            def probs_T1(t):
                wait(act, b_pTr, t.n + 1)
                wait(act, b_ctx, t.n)
                act.copy(pT1[:, 0:KT, :].rearrange("p (j i) n -> p j i n", i=2),
                         ps[:, 3:5, 256:512].rearrange("p j (i n) -> p j i n", i=2)).then_inc(b_pTa, 1)

            def high_ctx1(t):
                wait(act, b_ctx, t.n + 1)
                wait(act, b_wo, t.n)
                act.copy(yc[:, :, :], by_feature(bank(7))).then_inc(b_ch, 1)

            run_tiles(act, NT, [(softmax_exp1, 0), (latent, 1), (norm1, 2), (high_latent, 1),
                                (probs_T1, 0), (values1, 1), (queries_keys1, 1), (high_ctx1, 0), (high_y, 2)])


def kernel(x, pos_BxS, cond_2048, L0_cond_ln1_w, L0_cond_ln1_tw, L0_cond_ln2_w, L0_cond_ln2_tw,
           L0_cond_Wq, L0_cond_Wk, L0_cond_Wv, L0_cond_Wo, L0_cond_Wg, L0_cond_Wu, L0_cond_Wd,
           L1_cond_W_ada, L1_cond_b_ada, L1_cond_Wq, L1_cond_Wkd, L1_cond_Wku, L1_cond_Wvu, L1_cond_Wo):
    import concourse.bacc as bacc
    from concourse.bass_utils import run_bass_kernel_spmd

    B, T, D = x.shape
    turn = lambda a: np.ascontiguousarray(np.asarray(a).T)
    column = lambda a: turn(np.asarray(a).reshape(-1, 128))
    f32 = np.float32
    hd0, hd1 = 64, 32
    invf = (f32(1.0) / np.power(f32(10000.0), np.arange(0, hd0, 2, dtype=f32) / f32(hd0))).astype(f32)
    freq1 = (f32(1.0) / np.power(f32(10000.0), np.arange(0, hd1, 2, dtype=f32) / f32(hd1))).astype(f32)
    ang1 = np.arange(T, dtype=f32)[:, None] * freq1[None, :]
    cos1, sin1 = np.cos(ang1).astype(f32), np.sin(ang1).astype(f32)
    rope1 = np.stack([np.concatenate([cos1, cos1], 1), np.concatenate([-sin1, sin1], 1)], 1)
    arrays = {
        "x": np.ascontiguousarray(np.asarray(x).reshape(B * T, D)),
        "pos": turn(np.asarray(pos_BxS).reshape(B * T // 128, 128)),
        "condT": turn(cond_2048),
        "ln1_w": column(L0_cond_ln1_w), "ln1_twT": turn(L0_cond_ln1_tw),
        "ln2_w": column(L0_cond_ln2_w), "ln2_twT": turn(L0_cond_ln2_tw),
        "WqT": turn(L0_cond_Wq), "WkT": turn(L0_cond_Wk), "WvT": turn(L0_cond_Wv), "WoT": turn(L0_cond_Wo),
        "WgT": turn(L0_cond_Wg), "WuT": turn(L0_cond_Wu), "WdT": turn(L0_cond_Wd),
        "adaT": turn(L1_cond_W_ada), "b_ada": column(L1_cond_b_ada),
        "Wq1T": turn(L1_cond_Wq), "WkdT": turn(L1_cond_Wkd), "WkuT": turn(L1_cond_Wku),
        "WvuT": turn(L1_cond_Wvu), "Wo1T": turn(L1_cond_Wo),
        "invf": np.ascontiguousarray(np.broadcast_to(invf, (128, hd0 // 2))),
        "rope1": np.ascontiguousarray(np.concatenate([rope1] * (128 // T), 0)),
        "ident": np.eye(128, dtype=f32),
    }
    nc = bacc.Bacc("TRN2", target_bir_lowering=False, num_devices=1)
    args = [nc.dram_tensor(n, a.shape, mybir.dt.from_np(a.dtype), kind="ExternalInput").ap()
            for n, a in arrays.items()]
    out = nc.dram_tensor("out", (B * T, D), F32, kind="ExternalOutput").ap()
    build(nc, *args, out)
    r = run_bass_kernel_spmd(nc, [arrays], core_ids=[0])
    return r.results[0]["out"].reshape(B, T, D)
```

```python
from contextlib import ExitStack

import numpy as np
import concourse.bass as bass
from concourse import mybir

F32 = mybir.dt.float32
F32R = mybir.dt.float32r
I32 = mybir.dt.int32
ALU = mybir.AluOpType
ACT = mybir.ActivationFunctionType
AX_X = mybir.AxisListType.X

P = 128
S = 64
TB_TOKENS = 512


class Tile:

    def __init__(self, n, parity):
        self.n, self.par = n, parity % 2

    def at(self, shift):
        return Tile(self.n + shift, self.par + shift)


def wait(eng, sem, count):
    if isinstance(count, int) and count <= 0:
        return
    eng.wait_ge(sem, count)


def run_tiles(eng, n_tiles, stages, other=None):
    other = other or {}
    low = min(shift for _, shift in stages)
    high = max(shift for _, shift in stages)
    begin, end = -high, n_tiles - low
    loop_from = 2 - low + (2 - low) % 2
    loop_to = n_tiles - high
    loop_to -= loop_to % 2

    def step(t):
        for stage, shift in stages:
            u = t.at(shift)
            if isinstance(u.n, int) and not 0 <= u.n < n_tiles:
                continue
            stage(u)

    def steps_outside(t_from, t_to):
        for t in range(t_from, t_to):
            if t in other:
                other[t]()
            step(Tile(t, t))

    assert not any(loop_from <= t < loop_to for t in other)
    steps_outside(begin, loop_from)
    with eng.Fori(loop_from // 2, loop_to // 2) as pair:
        for k in range(2):
            step(Tile(pair * 2 + k, k))
    steps_outside(loop_to, end)


def build(nc, x, pos, condT, ln1_w, ln1_twT, ln2_w, ln2_twT, WqT, WkT, WvT, WoT, WgT, WuT, WdT,
          adaT, b_ada, Wq1T, WkdT, WkuT, WvuT, Wo1T, invf, rope1, ident, out):
    D = WqT.shape[0]
    KT = D // P
    NTOK = x.shape[0]
    NT = NTOK // P
    NB = NTOK // S
    INTER = WgT.shape[1]
    NG = INTER // P
    NBLK = NTOK // TB_TOKENS
    TPB = TB_TOKENS // P
    HD0, HD1 = WkT.shape[1], 32
    QK0 = (D + 2 * HD0) // 2
    QK1 = (D + P) // 2
    TWO_PI = 2 * np.pi
    C1 = 6.28125
    C2 = float(np.float32(np.round((TWO_PI - C1) * 2.0 ** 21) / 2.0 ** 21))
    C3 = float(np.float32(TWO_PI - C1 - C2))
    ROUND = 12582912.0

    with ExitStack() as ctx:
        def sb(name, shape, dt=F32, into=ctx):
            return into.enter_context(nc.sbuf_tensor(name, shape, dt))

        def sem(name):
            return ctx.enter_context(nc.semaphore(name))

        xres = sb("xres", [P, NT, D])
        wqh, wql = sb("wqh", [P, KT, 2 * QK0], F32R), sb("wql", [P, KT, 2 * QK0], F32R)
        woh, wol = sb("woh", [P, KT, D], F32R), sb("wol", [P, KT, D], F32R)
        kvh, kvl = sb("kvh", [P, 2 * P], F32R), sb("kvl", [P, 2 * P], F32R)
        sc_ln1, sc_ln2 = sb("sc_ln1", [P, KT, NB]), sb("sc_ln2", [P, KT, NB])
        sc_ada, sh_ada = sb("sc_ada", [P, KT, NB]), sb("sh_ada", [P, KT, NB])
        lnw = sb("lnw", [P, 2, KT])
        bada = sb("bada", [P, 2 * KT])
        idn = sb("idn", [P, P])
        condt = sb("condt", [P, KT, NB])
        rope1t = sb("rope1t", [P, 2, HD1])
        minus_half = sb("minus_half", [P, 1])
        stat = sb("stat", [P, 6, NT])

        ps = ctx.enter_context(nc.psum_tensor("ps", [P, 8, 512], F32))

        with ExitStack() as staged:
            wst = sb("wst", [P, KT, 2 * QK0], into=staged)
        yn, yf = sb("yn", [P, D]), sb("yf", [P, KT, P])
        qr1 = sb("qr1", [P, D])
        yh, yl = sb("yh", [P, KT, P], F32R), sb("yl", [P, KT, P], F32R)
        with ExitStack() as early:
            adaw = sb("adaw", [P, KT, 4 * D], into=early)
            wost = sb("wost", [P, KT, D], into=early)
        mlp = ExitStack()
        h2h = sb("h2h", [P, KT, NTOK], F32R, mlp)
        h2l = sb("h2l", [P, KT, NTOK], F32R, mlp)
        with ExitStack() as ropes:
            cos0, sin0 = sb("cos0", [P, NT, HD0], into=ropes), sb("sin0", [P, NT, HD0], into=ropes)
            t1, t2 = sb("t1", [P, 2, 5, HD0], into=ropes), sb("t2", [P, 2, 5, HD0], into=ropes)
        sg, af = sb("sg", [P, TB_TOKENS], into=mlp), sb("af", [P, TB_TOKENS], into=mlp)
        ah, al = [], []
        for i in range(2):
            ah.append(sb(f"ah{i}", [P, TB_TOKENS], F32R, mlp))
            al.append(sb(f"al{i}", [P, TB_TOKENS], F32R, mlp))
        sb("pad", [P, 2 * 10 * HD0 - 2 * TB_TOKENS], into=mlp)
        slot_shape = [P, 3, KT * P]
        mst = [sb("mst0", slot_shape, into=mlp)]
        mwh, mwl = [sb("mwh0", slot_shape, F32R, mlp)], [sb("mwl0", slot_shape, F32R, mlp)]
        with ExitStack() as l0:
            xn, xn2 = sb("xn", [P, D], into=l0), sb("xn2", [P, D], into=l0)
            hf, gf = sb("hf", [P, KT, P], into=l0), sb("gf", [P, KT, P], into=l0)
            hh, hl = sb("hh", [P, KT, P], F32R, l0), sb("hl", [P, KT, P], F32R, l0)
            qr = sb("qr", [P, 10 * HD0], into=l0)
            qT, kT = sb("qT", [P, KT, P], into=l0), sb("kT", [P, P], into=l0)
            ex = sb("ex", [P, KT, 2, S], into=l0)
            pT = sb("pT", [P, KT, P], into=l0)
            bdv = [sb(f"bdv{i}", [P, 2, 2 * HD0], into=l0) for i in range(2)]
            ch, cl = sb("ch", [P, KT, P], F32R, l0), sb("cl", [P, KT, P], F32R, l0)
            smx = sb("smx", [P, 3, 2 * KT], into=l0)
            posi, posf = sb("posi", [P, NT], I32, l0), sb("posf", [P, NT], into=l0)
            invt = sb("invt", [P, HD0 // 2], into=l0)
        mst.append(sb("mst1", slot_shape, into=mlp))
        mwh.append(sb("mwh1", slot_shape, F32R, mlp))
        mwl.append(sb("mwl1", slot_shape, F32R, mlp))
        mlp.close()
        u1, u2 = sb("u1", [P, 2, 10, HD1]), sb("u2", [P, 2, 10, HD1])
        lat, lath, latl = sb("lat", [P, P]), sb("lath", [P, P], F32R), sb("latl", [P, P], F32R)
        ku1, ku2, kr1 = sb("ku1", [P, KT, HD1]), sb("ku2", [P, KT, HD1]), sb("kr1", [P, KT, 4, HD1])
        qk1 = sb("qk1", [P, KT, 2, P])
        ex1 = sb("ex1", [P, KT, 4, S])
        pT1 = sb("pT1", [P, 2 * KT, P])
        bdv1 = [sb(f"bdv1_{i}", [P, 2, KT, 2 * HD1]) for i in range(2)]
        yc, ycl = sb("yc", [P, KT, P], F32R), sb("ycl", [P, KT, P], F32R)
        smx1 = sb("smx1", [P, 3, 4 * KT])
        bns = sb("bns", [P, 6])
        mv = [sb(f"mv{i}", [P, 2]) for i in range(2)]
        fin = [sb(f"fin{i}", [P, D]) for i in range(2)]

        (ld_pos, ld_cond, ld_x0, ld_idn, ld_ln1, ld_qkv, ld_wo, ld_x1, ld_x, ld_ada, ld_rope1) = [
            sem("ld_" + n) for n in "pos cond x0 idn ln1 qkv wo x1 x ada rope1".split()]
        ada_mm, ada_done, zeroed = sem("ada_mm"), sem("ada_done"), sem("zeroed")
        ang_step, ang_ready, rope_tab = sem("ang_step"), sem("ang_ready"), sem("rope_tab")
        w0h, w0l, w0ol = sem("w0h"), sem("w0l"), sem("w0ol")
        (a_ssq, a_ms, a_rstd, a_xn, a_xT, a_hf, a_hh, a_hl, a_qkv, a_rope, a_v, a_qr, a_qkT, a_qT, a_kT,
         a_sc, a_max, a_ds, a_ex, a_sum, a_rec, a_p, a_pTr, a_pT, a_ctx, a_ch, a_cl, a_wo, a_x,
         a_ssq2, a_ms2, a_rstd2, a_xn2, a_x2T, a_gf, a_h2h, a_h2l) = [sem("a_" + n) for n in (
            "ssq ms rstd xn xT hf hh hl qkv rope v qr qkT qT kT sc max ds ex sum rec p pTr pT ctx ch cl "
            "wo x ssq2 ms2 rstd2 xn2 x2T gf h2h h2l").split()]
        m_ld = [sem(f"m_ld{i}") for i in range(2)]
        (m_wh, m_wl, m_gate, m_up, m_sg, m_af, m_ah, m_al, m_down, m_x) = [sem("m_" + n) for n in (
            "wh wl gate up sg af ah al down x").split()]
        ld_l1, w1h, w1l = sem("ld_l1"), sem("w1h"), sem("w1l")
        (b_bn, b_mv, b_var, b_rstd, b_nb, b_xn, b_xT, b_yf, b_hh, b_hl, b_qc, b_rope, b_lat, b_qr,
         b_latT, b_lath, b_latl, b_kv, b_krope, b_kr, b_v, b_qkT, b_qka, b_qkb, b_sc, b_max, b_ds, b_ex,
         b_sum, b_rec, b_p, b_pTr, b_pTa, b_pTb, b_ctx, b_ch, b_cl, b_wo, b_out, b_zero) = [
            sem("b_" + n) for n in (
            "bn mv var rstd nb xn xT yf hh hl qc rope lat qr latT lath latl kv krope kr v qkT qT kT sc "
            "max ds ex sum rec p pTr pTa pTb ctx ch cl wo out zero").split()]
        b_st = [sem(f"b_st{i}") for i in range(2)]

        def bank(k):
            return ps[:, k, :]

        def by_feature(ap):
            return ap.rearrange("p (k n) -> p k n", k=KT)

        def by_entry(ap):
            return ap.rearrange("p k (b s) -> p k b s", b=2)

        def scale_of(tab, t):
            return tab[:, :, bass.ds(t.n * 2, 2)].unsqueeze(3).broadcast_to([P, KT, 2, S])

        def heads(k, hd):
            return ps[:, 1:3, 0:320].rearrange("p c (h d) -> p c h d", d=hd)

        wcols = {0: (WqT, WkT, WvT), 1: (Wq1T, WkdT)}

        def load_qkv(eng, dst, layer, signal):
            at = 0
            for w in wcols[layer]:
                n = w.shape[1]
                eng.dma_start(dst[:, :, at:at + n], w.rearrange("(k p) n -> p k n", p=P)).then_inc(signal, 16)
                at += n

        X1 = 6
        DOWN_BANKS = (5, 6, 7, 0)

        def upto(n):
            return min(n, NT) if isinstance(n, int) else n

        def y_bank(t):
            return bank(3) if isinstance(t.n, int) and t.n == 0 else bank(0)

        block = ctx.enter_context(nc.Block())

        @block.sync
        def _(sp):
            xv = x.rearrange("(t p) d -> p t d", p=P)
            for dst, src in ((posi[:, :], pos), (invt[:, :], invf)):
                sp.dma_start(dst, src).then_inc(ld_pos, 16)
            sp.dma_start(condt[:, :, :], condT.rearrange("(k p) b -> p k b", p=P)).then_inc(ld_cond, 16)
            sp.dma_start(lnw[:, 0, :], ln1_w).then_inc(ld_cond, 16)
            sp.dma_start(lnw[:, 1, :], ln2_w).then_inc(ld_cond, 16)
            sp.dma_start(bada[:, :], b_ada).then_inc(ld_cond, 16)
            sp.dma_start(xres[:, 0:2, :], xv[:, 0:2, :]).then_inc(ld_x0, 16)
            sp.dma_start(idn[:, :], ident).then_inc(ld_idn, 16)
            for w, at, signal in ((ln1_twT, 0, ld_ln1), (None, 0, None), (ln2_twT, D, ld_ada),
                                  (adaT, 2 * D, ld_ada)):
                if w is None:
                    load_qkv(sp, wst, 0, ld_qkv)
                    sp.dma_start(wost[:, :, :], WoT.rearrange("(k p) n -> p k n", p=P)).then_inc(ld_wo, 16)
                    sp.dma_start(xres[:, 2:X1, :], xv[:, 2:X1, :]).then_inc(ld_x1, 16)
                    continue
                sp.dma_start(adaw[:, :, at:at + w.shape[1]],
                             w.rearrange("(k p) n -> p k n", p=P)).then_inc(signal, 16)
            sp.dma_start(xres[:, X1:NT, :], xv[:, X1:NT, :]).then_inc(ld_x, 16)
            sp.dma_start(rope1t[:, :, :], rope1).then_inc(ld_rope1, 16)

            def load_group(g, slot, reused):
                if reused:
                    wait(sp, m_wh, g - 1)
                    wait(sp, m_wl, g - 1)
                for n, w in enumerate((WgT, WuT)):
                    sp.dma_start(mst[slot][:, n, :].rearrange("p (k m) -> p k m", k=KT),
                                 w[:, bass.ds(g * P, P)].rearrange("(k p) m -> p k m", p=P)
                                 ).then_inc(m_ld[slot], 16)
                sp.dma_start(mst[slot][:, 2, :], WdT[bass.ds(g * P, P), :]).then_inc(m_ld[slot], 16)

            def load_pairs(p_from, p_to):
                with sp.Fori(p_from, p_to) as pair:
                    for k in range(2):
                        load_group(pair * 2 + k, k, True)

            load_group(0, 0, False)
            wait(sp, a_h2l, NT)
            load_group(1, 1, False)
            load_qkv(sp, wst, 1, ld_l1)
            load_pairs(1, NG // 4 + 1)
            wait(sp, w1h, 1)
            wait(sp, w1l, 1)
            sp.dma_start(wst[:, 0:KT, 0:D], Wo1T.rearrange("(k p) n -> p k n", p=P)).then_inc(ld_l1, 16)
            sp.dma_start(wst[:, 0, D:D + P], WkuT).then_inc(ld_l1, 16)
            sp.dma_start(wst[:, 1, D:D + P], WvuT).then_inc(ld_l1, 16)
            load_pairs(NG // 4 + 1, NG // 2)
            with sp.Fori(0, NT // 2) as pair:
                for k in range(2):
                    t = pair * 2 + k
                    sp.wait_ge(b_out, t + 1)
                    sp.dma_start(out[bass.ds(t * P, P), :], fin[k][:, :]).then_inc(b_st[k], 16)
            for k in range(2):
                sp.wait_ge(b_st[k], 16 * (NT // 2))

        @block.gpsimd
        def _(pool):
            for i in range(2):
                pool.memset(bdv[i][:, :, :], 0.0).then_inc(zeroed, 1)
            pool.memset(minus_half[:, :], -0.5).then_inc(zeroed, 1)
            pool.wait_ge(zeroed, 3)

            def split_qkv():
                pool.wait_ge(w0h, 1)
                pool.tensor_tensor(wql[:, KT - 1, :], wst[:, KT - 1, :], wqh[:, KT - 1, :],
                                   ALU.subtract).then_inc(w0l, 1)

            def split_wo():
                pool.wait_ge(w0h, 2)
                pool.tensor_tensor(wol[:, :, :], wost[:, :, :], woh[:, :, :], ALU.subtract).then_inc(w0ol, 1)

            def inv_root(col, signal):
                pool.tensor_tensor(col, col, minus_half[:, :], ALU.pow).then_inc(signal, 1)

            def rstd(t):
                wait(pool, a_ms, t.n + 1)
                inv_root(stat[:, 1, bass.ds(t.n, 1)], a_rstd)

            def rstd2(t):
                wait(pool, a_ms2, t.n + 1)
                inv_root(stat[:, 3, bass.ds(t.n, 1)], a_rstd2)

            def low_h(t):
                wait(pool, a_hh, t.n + 1)
                wait(pool, a_qkv, t.n)
                pool.tensor_tensor(hl[:, :, :], hf[:, :, :], hh[:, :, :], ALU.subtract).then_inc(a_hl, 1)

            def rope_sum(t):
                wait(pool, a_rope, t.n + 1)
                wait(pool, a_qkT, t.n)
                u, v = (tile[:, :, :, :].rearrange("p c h d -> p (c h d)") for tile in (t1, t2))
                nk = D + HD0
                pool.tensor_tensor(qr[:, 0:nk], u[:, 0:nk], v[:, 0:nk], ALU.add)
                pool.tensor_tensor(qr[:, nk:nk + HD0], u[:, D:nk], v[:, D:nk], ALU.add).then_inc(a_qr, 1)

            def low_h2(t):
                wait(pool, a_h2h, t.n + 1)
                at = bass.ds(t.n * P, P)
                pool.tensor_tensor(h2l[:, :, at], gf[:, :, :], h2h[:, :, at], ALU.subtract).then_inc(a_h2l, 1)

            def split_group(g, slot):
                pool.wait_ge(m_wh, g + 1)
                pool.tensor_tensor(mwl[slot][:, :, :], mst[slot][:, :, :], mwh[slot][:, :, :],
                                   ALU.subtract).then_inc(m_wl, 1)

            def split_pairs(p_from, p_to):
                with pool.Fori(p_from, p_to) as pair:
                    for k in range(2):
                        split_group(pair * 2 + k, k)

            run_tiles(pool, NT, [(rstd, 3), (low_h, 2), (rope_sum, 1), (low_h2, -2), (rstd2, -1)],
                      {-1: split_qkv, 0: split_wo, 13: lambda: split_group(0, 0)})
            split_group(1, 1)
            split_pairs(1, NG // 4)
            split_group(NG // 2, 0)
            pool.wait_ge(w1h, 1)
            pool.tensor_tensor(wql[:, :, :], wst[:, :, :], wqh[:, :, :], ALU.subtract).then_inc(w1l, 1)
            split_group(NG // 2 + 1, 1)
            split_pairs(NG // 4 + 1, NG * 3 // 8)
            split_group(NG * 3 // 4, 0)
            pool.wait_ge(w1h, 3)
            pool.tensor_tensor(wol[:, :, :], wst[:, :, 0:D], woh[:, :, :], ALU.subtract).then_inc(w1l, 1)
            pool.tensor_tensor(kvl[:, :].rearrange("p (c n) -> p c n", c=2), wst[:, 0:2, D:D + P],
                               kvh[:, :].rearrange("p (c n) -> p c n", c=2), ALU.subtract).then_inc(w1l, 1)
            split_group(NG * 3 // 4 + 1, 1)
            split_pairs(NG * 3 // 8 + 1, NG // 2)

            def rstd1(t):
                wait(pool, b_var, t.n + 1)
                inv_root(stat[:, 4, bass.ds(t.n, 1)], b_rstd)

            def low_y(t):
                wait(pool, b_hh, t.n + 1)
                wait(pool, b_qc, 2 * t.n)
                pool.tensor_tensor(yl[:, :, :], yf[:, :, :], yh[:, :, :], ALU.subtract).then_inc(b_hl, 1)

            def rope_sum1(t):
                wait(pool, b_rope, t.n + 1)
                wait(pool, b_qkT, t.n)
                pool.tensor_tensor(qr1[:, :], u1[:, :, :, :].rearrange("p c h d -> p (c h d)")[:, 0:D],
                                   u2[:, :, :, :].rearrange("p c h d -> p (c h d)")[:, 0:D],
                                   ALU.add).then_inc(b_qr, 1)

            def clear_bdv1():
                pool.wait_ge(m_x, NG * NT)
                for i in range(2):
                    pool.memset(bdv1[i][:, :, :, :], 0.0).then_inc(b_zero, 1)

            run_tiles(pool, NT, [(rstd1, 4), (rope_sum1, 2), (low_y, 3)], {-2: clear_bdv1})

        @block.tensor
        def _(pe):
            def three(dst, lh, ll, rh, rl, start, stop):
                pe.matmul(dst, lh, rh, start=start, stop=False)
                pe.matmul(dst, ll, rh, start=False, stop=False)
                return pe.matmul(dst, lh, rl, start=False, stop=stop)

            def adaptive(m_from, m_to, to_bank):
                for m in range(m_from, m_to):
                    for k in range(KT):
                        mm = pe.matmul(ps[:, to_bank, NB * m:NB * (m + 1)], adaw[:, k, P * m:P * (m + 1)],
                                       condt[:, k, :], start=(k == 0), stop=(k == KT - 1))
                mm.then_inc(ada_mm, 1)

            pe.wait_ge(ld_cond, 64)
            pe.wait_ge(ld_ln1, 16)
            adaptive(0, KT, 1)
            pe.wait_ge(ld_idn, 16)

            def adaptive_rest():
                pe.wait_ge(ld_ada, 32)
                adaptive(KT, 4 * KT, 7)

            def x_T(t):
                wait(pe, a_xn, t.n + 1)
                wait(pe, a_hf, t.n)
                wait(pe, a_gf, t.n - 4)
                for k in range(KT):
                    if k == KT - 1:
                        scores_free(t.at(-2))
                    mm = pe.transpose(ps[:, 0, P * k:P * (k + 1)], xn[:, P * k:P * (k + 1)], idn[:, :])
                mm.then_inc(a_xT, 1)

            def scores_free(t):
                if isinstance(t.n, int) and t.n < 0:
                    return
                wait(pe, a_qT, t.n + 1)
                wait(pe, a_kT, t.n + 1)

            def qkv(t):
                if isinstance(t.n, int) and t.n == 0:
                    pe.wait_ge(w0h, 1)
                    pe.wait_ge(w0l, 2)
                    pe.wait_ge(ada_done, 1)
                wait(pe, a_hh, t.n + 1)
                wait(pe, a_hl, t.n + 1)
                wait(pe, a_rope, t.n)
                wait(pe, a_v, t.n)
                for c in range(2):
                    cols = slice(QK0 * c, QK0 * (c + 1))
                    for k in range(KT):
                        mm = three(ps[:, 1 + c, 0:QK0], hh[:, k, :], hl[:, k, :], wqh[:, k, cols],
                                   wql[:, k, cols], k == 0, k == KT - 1)
                mm.then_inc(a_qkv, 1)

            def qk_T(t):
                wait(pe, a_qr, t.n + 1)
                wait(pe, a_pT, t.n)
                wait(pe, a_ds, t.n)
                for k in range(KT):
                    pe.transpose(ps[:, 5, P * k:P * (k + 1)], qr[:, P * k:P * (k + 1)], idn[:, :])
                mm = pe.transpose(ps[:, 3, 256:384], qr[:, D:D + 2 * HD0], idn[:, :])
                mm.then_inc(a_qkT, 1)

            def scores(t):
                if isinstance(t.n, int) and t.n >= NT - 2:
                    scores_free(t)
                for j in range(KT):
                    for b in range(2):
                        for i in range(2):
                            r, q = slice(HD0 * i, HD0 * (i + 1)), slice(S * b, S * (b + 1))
                            mm = pe.matmul(ps[q, 3 + i, S * j:S * (j + 1)], qT[r, j, q], kT[r, q],
                                           start=True, stop=True)
                mm.then_inc(a_sc, 1)

            def p_T(t):
                wait(pe, a_p, t.n + 1)
                wait(pe, a_qT, t.n + 1)
                for j in range(KT):
                    mm = pe.transpose(ps[:, 5, P * j:P * (j + 1)],
                                      ex[:, j, :, :].rearrange("p i s -> p (i s)"), idn[:, :])
                mm.then_inc(a_pTr, 1)

            def context(t):
                wait(pe, a_pT, t.n + 1)
                wait(pe, a_v, t.n + 1)
                wait(pe, a_ch, t.n)
                wait(pe, a_cl, t.n)
                for b in range(2):
                    mm = pe.matmul(ps[:, 6, 256 * b:256 * (b + 1)], bdv[t.par][:, b, :],
                                   pT[:, :, S * b:S * (b + 1)], start=True, stop=True)
                mm.then_inc(a_ctx, 1)

            def project(t):
                if isinstance(t.n, int) and t.n == 0:
                    pe.wait_ge(w0ol, 1)
                    pe.wait_ge(ada_done, 4)
                wait(pe, a_ch, t.n + 1)
                wait(pe, a_cl, t.n + 1)
                wait(pe, a_x, t.n)
                for k in range(KT):
                    mm = three(bank(7), ch[:, k, :], cl[:, k, :], woh[:, k, :], wol[:, k, :],
                               k == 0, k == KT - 1)
                mm.then_inc(a_wo, 1)

            def x2_T(t):
                wait(pe, a_xn2, t.n + 1)
                wait(pe, a_gf, t.n)
                wait(pe, a_hf, min(t.n + 5, NT) if isinstance(t.n, int) else t.n + 5)
                for k in range(KT):
                    mm = pe.transpose(ps[:, 0, P * k:P * (k + 1)], xn2[:, P * k:P * (k + 1)], idn[:, :])
                mm.then_inc(a_x2T, 1)


            def gate_up(g, r, slot, first):
                n = g * NBLK + r
                if r == 0:
                    pe.wait_ge(m_wl, g + 1)
                if first:
                    pe.wait_ge(a_h2l, TPB * (r + 1))
                    pe.wait_ge(a_h2h, TPB * (r + 1))
                wait(pe, m_sg, n - 1)
                wait(pe, m_af, n - 1)
                tok = slice(TB_TOKENS * r, TB_TOKENS * (r + 1))
                for w, done in ((0, m_gate), (1, m_up)):
                    for k in range(KT):
                        f = slice(P * k, P * (k + 1))
                        mm = three(bank(1 + 2 * w + r % 2), mwh[slot][:, w, f], mwl[slot][:, w, f],
                                   h2h[:, k, tok], h2l[:, k, tok], k == 0, k == KT - 1)
                    mm.then_inc(done, 1)

            def down(n, act, slot):
                pe.wait_ge(m_al, n + 1)
                for i in range(TPB):
                    wait(pe, m_x, (n - 1) * TPB + i + 1)
                    f = slice(P * i, P * (i + 1))
                    three(bank(DOWN_BANKS[i]), ah[act][:, f], al[act][:, f], mwh[slot][:, 2, :],
                          mwl[slot][:, 2, :], True, True).then_inc(m_down, 1)

            def group(g, slot):
                for r in range(NBLK):
                    gate_up(g, r, slot, False)
                    down(g * NBLK + (r - 1), (r - 1) % 2, slot if r else 1 - slot)

            run_tiles(pe, NT, [(x_T, 2), (scores, 0), (qkv, 1), (x2_T, -2), (p_T, 0),
                               (project, -1), (qk_T, 1), (context, 0)],
                      {0: adaptive_rest, NT: lambda: gate_up(0, 0, 0, True),
                       NT + 1: lambda: gate_up(0, 1, 0, True)})
            pe.wait_ge(a_gf, NT)
            down(0, 0, 0)
            for r in range(2, NBLK):
                gate_up(0, r, 0, True)
                down(r - 1, (r - 1) % 2, 0)
            with pe.Fori(0, NG // 2 - 1) as pair:
                group(pair * 2 + 1, 1)
                group(pair * 2 + 2, 0)
            group(NG - 1, 1)

            def y_T(t):
                wait(pe, b_xn, t.n + 1)
                if isinstance(t.n, int) and t.n == 0:
                    pe.wait_ge(m_af, NG * NBLK - 1)
                else:
                    wait(pe, b_yf, t.n)
                    wait(pe, b_ch, t.n - 3)
                    wait(pe, b_cl, t.n - 3)
                for k in range(KT):
                    mm = pe.transpose(y_bank(t)[:, P * k:P * (k + 1)], yn[:, P * k:P * (k + 1)], idn[:, :])
                mm.then_inc(b_xT, 1)

            def attention1_after_down():
                down(NG * NBLK - 1, 1, 1)
                pe.wait_ge(w1l, 3)
                pe.wait_ge(m_x, NG * NT)

            def q_latent(t, c):
                cols = slice(QK1 * c, QK1 * (c + 1))
                for k in range(KT):
                    mm = three(ps[:, 1 + c, 0:QK1], yh[:, k, :], yl[:, k, :], wqh[:, k, cols],
                               wql[:, k, cols], k == 0, k == KT - 1)
                mm.then_inc(b_qc, 1)

            def q_latent_upper(t):
                wait(pe, b_hl, t.n + 1)
                wait(pe, b_rope, t.n)
                wait(pe, b_krope, t.n)
                wait(pe, b_v, t.n)
                q_latent(t, 1)

            def q_latent_lower(t):
                q_latent(t, 0)

            def latent_T(t):
                wait(pe, b_lat, t.n + 1)
                wait(pe, b_qka, upto(t.n))
                pe.transpose(ps[:, 3, 256:384], lat[:, :], idn[:, :]).then_inc(b_latT, 1)

            def keys_values(t):
                wait(pe, b_latl, t.n + 1)
                for c in range(2):
                    cols = slice(P * c, P * (c + 1))
                    mm = three(ps[:, 1 + c, QK1:QK1 + P], lath[:, :], latl[:, :], kvh[:, cols],
                               kvl[:, cols], True, True)
                mm.then_inc(b_kv, 1)

            def qk_T1(t):
                wait(pe, b_qr, t.n + 1)
                wait(pe, b_kr, t.n + 1)
                wait(pe, b_ds, 2 * t.n)
                for j in range(KT):
                    pe.transpose(ps[:, 3 + j, 256:384], qr1[:, P * j:P * (j + 1)], idn[:, :])
                    mm = pe.transpose(ps[:, 3 + j, 384:512],
                                      kr1[:, j, :, :].rearrange("p g d -> p (g d)"), idn[:, :])
                mm.then_inc(b_qkT, 1)

            def scores1(t):
                wait(pe, b_qka, t.n + 1)
                wait(pe, b_qkb, t.n + 1)
                for j in range(KT):
                    for b in range(2):
                        for g in range(4):
                            r, q = slice(HD1 * g, HD1 * (g + 1)), slice(S * b, S * (b + 1))
                            mm = pe.matmul(ps[q, 3 + g, S * j:S * (j + 1)], qk1[r, j, 0, q], qk1[r, j, 1, q],
                                           start=True, stop=True, tile_position=(HD1 * g, S * b))
                mm.then_inc(b_sc, 1)

            def p_T1(t):
                wait(pe, b_p, t.n + 1)
                wait(pe, b_qka, upto(t.n + 2))
                wait(pe, b_qkb, upto(t.n + 2))
                wait(pe, b_latl, upto(t.n + 3))
                for j in range(KT):
                    for i in range(2):
                        mm = pe.transpose(ps[:, 3 + j, 256 + P * i:256 + P * (i + 1)],
                                          ex1[:, j, 2 * i:2 * i + 2, :].rearrange("p g s -> p (g s)"), idn[:, :])
                mm.then_inc(b_pTr, 1)

            def context1(t):
                wait(pe, b_pTa, t.n + 1)
                wait(pe, b_pTb, t.n + 1)
                wait(pe, b_v, t.n + 1)
                wait(pe, b_yf, upto(t.n + 4))
                for j in range(KT):
                    for b in range(2):
                        for i in range(2):
                            mm = pe.matmul(ps[S * i:S * (i + 1), 0, P * j + S * b:P * j + S * (b + 1)],
                                           bdv1[t.par][:, b, j, :], pT1[:, 2 * j + i, S * b:S * (b + 1)],
                                           start=True, stop=True)
                mm.then_inc(b_ctx, 1)

            def project1(t, k_from, k_to):
                for k in range(k_from, k_to):
                    mm = three(bank(7), yc[:, k, :], ycl[:, k, :], woh[:, k, :], wol[:, k, :],
                               k == 0, k == KT - 1)
                return mm

            def project1_begin(t):
                wait(pe, b_ch, t.n + 1)
                wait(pe, b_cl, t.n + 1)
                wait(pe, b_out, t.n)
                project1(t, 0, KT - 2)

            def project1_middle(t):
                project1(t, KT - 2, KT - 1)

            def project1_end(t):
                project1(t, KT - 1, KT).then_inc(b_wo, 1)

            run_tiles(pe, NT, [(scores1, 0), (q_latent_upper, 2), (y_T, 3), (q_latent_lower, 2),
                               (qk_T1, 1), (project1_begin, -1), (latent_T, 2), (project1_middle, -1),
                               (p_T1, 0), (keys_values, 2), (context1, 0), (project1_end, -1)],
                      {-2: attention1_after_down})

        @block.vector
        def _(dve):
            dve.wait_ge(ld_pos, 32)
            dve.tensor_copy(posf[:, :], posi[:, :]).then_inc(ang_step, 1)
            NA = HD0 // 2
            flat = lambda tile: tile[:, :, :, :].rearrange("p c h d -> p (c h d)")[:, 0:NT * NA]
            angle, turns, red = flat(t1), flat(t2), flat(ex)
            dve.wait_ge(ang_step, 1)
            dve.tensor_tensor(angle.rearrange("p (t a) -> p t a", t=NT),
                              posf[:, :].unsqueeze(2).broadcast_to([P, NT, NA]),
                              invt[:, :].unsqueeze(1).broadcast_to([P, NT, NA]), ALU.mult).then_inc(ang_step, 1)
            dve.wait_ge(ang_step, 2)
            dve.tensor_scalar(turns, angle, 1.0 / TWO_PI, ROUND, ALU.mult, ALU.add).then_inc(ang_step, 1)
            dve.wait_ge(ang_step, 3)
            dve.tensor_scalar(turns, turns, -ROUND, None, ALU.add).then_inc(ang_step, 1)
            step = 4
            src = angle
            for part in (C1, C2, C3):
                dve.wait_ge(ang_step, step)
                dve.scalar_tensor_tensor(out=red, in0=turns, scalar=-part, in1=src, op0=ALU.mult,
                                         op1=ALU.add).then_inc(ang_step, 1)
                src = red
                step += 1
            dve.wait_ge(ang_step, step)
            dve.tensor_scalar(red, red, float(np.float32(3.1415925)), -float(np.float32(3.1415925)),
                              ALU.min, ALU.max).then_inc(ang_step, 1)
            dve.wait_ge(ang_step, step + 1)
            dve.scalar_tensor_tensor(out=angle, in0=red, scalar=-1.0, in1=red, op0=ALU.mult,
                                     op1=ALU.max).then_inc(ang_step, 1)
            dve.wait_ge(ang_step, step + 2)
            dve.tensor_scalar(angle, angle, -1.0, float(np.pi / 2), ALU.mult, ALU.add).then_inc(ang_ready, 1)


            def adaptive_scale(n, tab, from_bank):
                for k in range(KT):
                    ins = dve.tensor_scalar(tab[:, k, :], ps[:, from_bank, NB * (KT * n + k):NB * (KT * n + k + 1)],
                                            1.0, lnw[:, n, k:k + 1], ALU.add, ALU.mult)
                ins.then_inc(ada_done, 1)

            def adaptive_first():
                dve.wait_ge(ada_mm, 1)
                adaptive_scale(0, sc_ln1, 1)
                dve.wait_ge(ada_done, 1)

            def split_qkv():
                dve.wait_ge(w0h, 1)
                dve.tensor_tensor(wql[:, 0:KT - 1, :], wst[:, 0:KT - 1, :], wqh[:, 0:KT - 1, :],
                                  ALU.subtract).then_inc(w0l, 1)
                dve.wait_ge(rope_tab, 4)

            def adaptive_rest():
                dve.wait_ge(ada_mm, 2)
                adap = lambda m: ps[:, 7, NB * m:NB * (m + 1)]
                adaptive_scale(1, sc_ln2, 7)
                for k in range(KT):
                    ins = dve.tensor_scalar(sc_ada[:, k, :], adap(2 * KT + k), bada[:, k:k + 1], 1.0,
                                            ALU.add, ALU.add)
                ins.then_inc(ada_done, 1)
                for k in range(KT):
                    ins = dve.tensor_scalar(sh_ada[:, k, :], adap(3 * KT + k), bada[:, KT + k:KT + k + 1],
                                            None, ALU.add)
                ins.then_inc(ada_done, 1)
                dve.wait_ge(ada_done, 4)

            def mean_sq(t):
                wait(dve, a_ssq, t.n + 1)
                dve.tensor_scalar(stat[:, 1, bass.ds(t.n, 1)], stat[:, 0, bass.ds(t.n, 1)], 1e-6, None,
                                  ALU.add).then_inc(a_ms, 1)

            def mean_sq2(t):
                wait(dve, a_ssq2, t.n + 1)
                dve.tensor_scalar(stat[:, 3, bass.ds(t.n, 1)], stat[:, 2, bass.ds(t.n, 1)], 1e-6, None,
                                  ALU.add).then_inc(a_ms2, 1)

            def scale_h(t):
                wait(dve, a_xT, t.n + 1)
                wait(dve, a_hl, t.n)
                dve.tensor_tensor(by_entry(hf[:, :, :]), by_entry(by_feature(bank(0))), scale_of(sc_ln1, t),
                                  ALU.mult).then_inc(a_hf, 1)

            def scale_h2(t):
                wait(dve, a_x2T, t.n + 1)
                wait(dve, a_h2l, t.n)
                dve.tensor_tensor(by_entry(gf[:, :, :]), by_entry(by_feature(bank(0))), scale_of(sc_ln2, t),
                                  ALU.mult).then_inc(a_gf, 1)

            def rope_mul(t):
                wait(dve, a_qkv, t.n + 1)
                wait(dve, a_qr, t.n)
                q, half = heads(0, HD0), HD0 // 2
                tab = lambda m, a, b: (m[:, bass.ds(t.n, 1), a:b].unsqueeze(1)
                                       .broadcast_to([P, 2, 5, b - a]))
                dve.tensor_tensor(t1[:, :, :, :], q, tab(cos0, 0, HD0), ALU.mult)
                dve.tensor_tensor(t2[:, :, :, 0:half], q[:, :, :, half:HD0], tab(sin0, 0, half), ALU.mult)
                dve.tensor_tensor(t2[:, :, :, half:HD0], q[:, :, :, 0:half], tab(sin0, half, HD0),
                                  ALU.mult).then_inc(a_rope, 1)

            def keys(t):
                wait(dve, a_qkT, t.n + 1)
                wait(dve, a_sc, t.n)
                dve.tensor_copy(kT[:, :], ps[:, 3, 256:384]).then_inc(a_kT, 1)

            def sc_view():
                return ps[:, 3:5, 0:256].rearrange("p i (j s) -> p i j s", j=KT)

            def ex_view():
                return ex[:, :, :, :].rearrange("p j i s -> p i j s")

            def row(n):
                return (smx[:, n, :].rearrange("p (i j) -> p i j", i=2).unsqueeze(3)
                        .broadcast_to([P, 2, KT, S]))

            def softmax_sub(t):
                wait(dve, a_sc, t.n + 1)
                wait(dve, a_pTr, t.n)
                dve.tensor_reduce(smx[:, 0, :].rearrange("p (i j) -> p i j", i=2), sc_view(), AX_X,
                                  ALU.max).then_inc(a_max, 1)
                wait(dve, a_max, t.n + 1)
                dve.tensor_tensor(ex_view(), sc_view(), row(0), ALU.subtract).then_inc(a_ds, 1)

            def softmax_norm(t):
                wait(dve, a_ex, t.n + 1)
                dve.tensor_reduce(smx[:, 1, :].rearrange("p (i j) -> p i j", i=2), ex_view(), AX_X,
                                  ALU.add).then_inc(a_sum, 1)
                wait(dve, a_sum, t.n + 1)
                dve.reciprocal(smx[:, 2, :], smx[:, 1, :]).then_inc(a_rec, 1)
                wait(dve, a_rec, t.n + 1)
                dve.tensor_tensor(ex_view(), ex_view(), row(2), ALU.mult).then_inc(a_p, 1)

            def low_ctx(t):
                wait(dve, a_ch, t.n + 1)
                wait(dve, a_wo, t.n)
                dve.tensor_tensor(by_entry(cl[:, :, :]), bank(6).rearrange("p (b j s) -> p j b s", b=2, j=KT),
                                  by_entry(ch[:, :, :]), ALU.subtract).then_inc(a_cl, 1)

            def add_x(t):
                wait(dve, a_wo, t.n + 1)
                at = xres[:, bass.ds(t.n, 1), :].rearrange("p o d -> p (o d)")
                dve.tensor_tensor(at, bank(7), at, ALU.add).then_inc(a_x, 1)

            def mlp_step(g, r):
                n = g * NBLK + r
                dve.wait_ge(m_sg, n + 1)
                dve.wait_ge(m_up, n + 1)
                wait(dve, m_al, n)
                wait(dve, m_ah, n)
                dve.tensor_tensor(af[:, :], bank(3 + r % 2), sg[:, :], ALU.mult).then_inc(m_af, 1)
                dve.wait_ge(m_ah, n + 1)
                wait(dve, m_down, TPB * (n - 1))
                dve.tensor_tensor(al[r % 2][:, :], af[:, :], ah[r % 2][:, :], ALU.subtract).then_inc(m_al, 1)

            def add_block(g, r):
                for i in range(TPB):
                    dve.wait_ge(m_down, (g * NBLK + r) * TPB + i + 1)
                    at = xres[:, TPB * (r % NBLK) + i, :]
                    dve.tensor_tensor(at, bank(DOWN_BANKS[i]), at, ALU.add).then_inc(m_x, 1)

            def mlp_group(g):
                for r in range(NBLK):
                    mlp_step(g, r)
                    add_block(g, r - 1)

            run_tiles(dve, NT, [(mean_sq, 3), (softmax_sub, 0), (scale_h, 2), (softmax_norm, 0), (rope_mul, 1),
                                (scale_h2, -2), (add_x, -1), (keys, 1), (mean_sq2, -1), (low_ctx, 0)],
                      {-2: adaptive_first, -1: split_qkv, 0: adaptive_rest, NT: lambda: mlp_step(0, 0), NT + 1: lambda: mlp_step(0, 1)})
            add_block(0, 0)
            for r in range(2, NBLK):
                mlp_step(0, r)
                add_block(0, r - 1)
            with dve.Fori(1, NG) as g:
                mlp_group(g)

            def stats1(t):
                wait(dve, b_xn, t.n)
                at = lambda n: stat[:, n, bass.ds(t.n, 1)]
                m = mv[t.par]
                dve.bn_stats(bns[:, :], xres[:, bass.ds(t.n, 1), :].rearrange("p o d -> p (o d)")
                             ).then_inc(b_bn, 1)

            def stats1_there(t):
                wait(dve, b_bn, t.n + 1)

            def mean_var(t):
                m, at = mv[t.par], lambda n: stat[:, n, bass.ds(t.n, 1)]
                dve.bn_aggr(m[:, :], bns[:, :]).then_inc(b_mv, 1)
                wait(dve, b_mv, t.n + 1)
                dve.tensor_scalar(at(4), m[:, 1:2], 1e-5, None, ALU.add).then_inc(b_var, 1)

            def mean_rstd(t):
                m, at = mv[t.par], lambda n: stat[:, n, bass.ds(t.n, 1)]
                wait(dve, b_rstd, t.n + 1)
                dve.scalar_tensor_tensor(out=at(5), in0=m[:, 0:1], scalar=-1.0, in1=at(4), op0=ALU.mult,
                                         op1=ALU.mult).then_inc(b_nb, 1)

            half1 = HD1 // 2

            def tab1(m, a, b, n):
                return rope1t[:, m, a:b].unsqueeze(1).unsqueeze(1).broadcast_to([P, n[0], n[1], b - a])

            def rope_mul1(t):
                wait(dve, b_kv, t.n + 1)
                wait(dve, b_qr, t.n)
                q = heads(0, HD1)
                dve.tensor_tensor(u1[:, :, :, :], q, tab1(0, 0, HD1, (2, 10)), ALU.mult)
                dve.tensor_tensor(u2[:, :, :, 0:half1], q[:, :, :, half1:HD1], tab1(1, 0, half1, (2, 10)),
                                  ALU.mult)
                dve.tensor_tensor(u2[:, :, :, half1:HD1], q[:, :, :, 0:half1], tab1(1, half1, HD1, (2, 10)),
                                  ALU.mult).then_inc(b_rope, 1)

            def low_latent(t):
                wait(dve, b_lath, t.n + 1)
                wait(dve, b_kv, t.n)
                dve.tensor_tensor(latl[:, :], ps[:, 3, 256:384], lath[:, :], ALU.subtract).then_inc(b_latl, 1)

            def key_rope(t):
                wait(dve, b_kv, t.n + 1)
                wait(dve, b_kr, t.n)
                wait(dve, b_qkT, t.n)
                k = ps[:, 1, QK1:QK1 + P].rearrange("p (j d) -> p j d", j=KT)
                tab = lambda m, a, b: rope1t[:, m, a:b].unsqueeze(1).broadcast_to([P, KT, b - a])
                dve.tensor_tensor(ku1[:, :, :], k, tab(0, 0, HD1), ALU.mult)
                dve.tensor_tensor(ku2[:, :, 0:half1], k[:, :, half1:HD1], tab(1, 0, half1), ALU.mult)
                dve.tensor_tensor(ku2[:, :, half1:HD1], k[:, :, 0:half1], tab(1, half1, HD1),
                                  ALU.mult).then_inc(b_krope, 1)
                wait(dve, b_krope, t.n + 1)
                rep = lambda tile: tile[:, :, :].unsqueeze(2).broadcast_to([P, KT, 4, HD1])
                dve.tensor_tensor(kr1[:, :, :, :], rep(ku1), rep(ku2), ALU.add).then_inc(b_kr, 1)

            def sc_view1():
                return ps[:, 3:7, 0:256].rearrange("p g (j s) -> p g j s", j=KT)

            def ex_view1():
                return ex1[:, :, :, :].rearrange("p j g s -> p g j s")

            def max_view1(n):
                return smx1[:, n, :].rearrange("p (g j) -> p g j", g=4)

            def softmax_sub1(t):
                wait(dve, b_sc, t.n + 1)
                wait(dve, b_pTr, t.n)
                dve.tensor_reduce(max_view1(0), sc_view1(), AX_X, ALU.max).then_inc(b_max, 1)
                wait(dve, b_max, t.n + 1)
                for g in (slice(0, 2), slice(2, 4)):
                    dve.tensor_tensor(ex_view1()[:, g], sc_view1()[:, g], max_view1(0)[:, g].unsqueeze(3)
                                      .broadcast_to([P, 2, KT, S]), ALU.subtract).then_inc(b_ds, 1)

            def softmax_norm1(t):
                for i, g in enumerate((slice(0, 2), slice(2, 4))):
                    wait(dve, b_ex, 2 * t.n + i + 1)
                    dve.tensor_reduce(max_view1(1)[:, g], ex_view1()[:, g], AX_X, ALU.add).then_inc(b_sum, 1)
                wait(dve, b_sum, 2 * t.n + 2)
                dve.reciprocal(smx1[:, 2, :], smx1[:, 1, :]).then_inc(b_rec, 1)
                wait(dve, b_rec, t.n + 1)
                dve.tensor_tensor(ex_view1(), ex_view1(), max_view1(2).unsqueeze(3)
                                  .broadcast_to([P, 4, KT, S]), ALU.mult).then_inc(b_p, 1)

            def queries_keys1(t):
                wait(dve, b_qkT, t.n + 1)
                wait(dve, b_sc, t.n)
                dve.tensor_copy(qk1[:, 2:4, :, :], ps[:, 5:7, 256:512].rearrange("p j (c n) -> p j c n", c=2)
                                ).then_inc(b_qkb, 1)

            def probs_T1(t):
                wait(dve, b_pTr, t.n + 1)
                wait(dve, b_ctx, t.n)
                dve.tensor_copy(pT1[:, KT:2 * KT, :].rearrange("p (j i) n -> p j i n", i=2),
                                ps[:, 5:7, 256:512].rearrange("p j (i n) -> p j i n", i=2)).then_inc(b_pTb, 1)

            def low_ctx1(t):
                wait(dve, b_ch, t.n + 1)
                wait(dve, b_wo, t.n)
                dve.tensor_tensor(ycl[:, :, :], by_feature(bank(0)), yc[:, :, :], ALU.subtract).then_inc(b_cl, 1)

            def add_out(t):
                wait(dve, b_wo, t.n + 1)
                wait(dve, b_st[t.par], (t.n - t.par) * 8)
                dve.tensor_tensor(fin[t.par][:, :], bank(7), xres[:, bass.ds(t.n, 1), :].rearrange(
                    "p o d -> p (o d)"), ALU.add).then_inc(b_out, 1)

            def mlp_sums():
                add_block(NG - 1, NBLK - 1)
                dve.wait_ge(ld_rope1, 16)

            run_tiles(dve, NT, [(softmax_sub1, 0), (softmax_norm1, 0), (queries_keys1, 1), (stats1, 4),
                                (stats1_there, 4), (low_latent, 2), (mean_var, 4), (probs_T1, 0),
                                (mean_rstd, 4), (rope_mul1, 2), (key_rope, 2), (add_out, -1),
                                (low_ctx1, 0)],
                      {-2: mlp_sums})

        @block.scalar
        def _(act):
            NA = HD0 // 2
            flat = lambda tile: (tile[:, :, :, :].rearrange("p c h d -> p (c h d)")[:, 0:NT * NA]
                                 .rearrange("p (t a) -> p t a", t=NT))
            act.wait_ge(ang_ready, 1)
            act.activation(sin0[:, :, 0:NA], flat(ex), ACT.Sin, scale=-1.0).then_inc(rope_tab, 1)
            act.activation(sin0[:, :, NA:HD0], flat(ex), ACT.Sin).then_inc(rope_tab, 1)
            act.activation(cos0[:, :, 0:NA], flat(t1), ACT.Sin).then_inc(rope_tab, 1)
            act.activation(cos0[:, :, NA:HD0], flat(t1), ACT.Sin).then_inc(rope_tab, 1)
            act.wait_ge(ld_x0, 16)

            def split_qkv():
                act.wait_ge(ld_qkv, 48)
                act.copy(wqh[:, :, :], wst[:, :, :]).then_inc(w0h, 1)

            def split_wo():
                act.wait_ge(ld_wo, 16)
                act.copy(woh[:, :, :], wost[:, :, :]).then_inc(w0h, 1)
                act.wait_ge(ld_x1, 16)

            def rest_of_x():
                act.wait_ge(ld_x, 16)
            act.wait_ge(zeroed, 2)

            def xt(t):
                return xres[:, bass.ds(t.n, 1), :].rearrange("p o d -> p (o d)")

            def square(t):
                wait(act, a_xT, t.n)
                act.activation(xn[:, :], xt(t), ACT.Square, scale=float(D) ** -0.5,
                               accum_out=stat[:, 0, bass.ds(t.n, 1)]).then_inc(a_ssq, 1)

            def norm(t):
                wait(act, a_rstd, t.n + 1)
                act.activation(xn[:, :], xt(t), ACT.Copy, scale=stat[:, 1, bass.ds(t.n, 1)]).then_inc(a_xn, 1)

            def high_h(t):
                wait(act, a_hf, t.n + 1)
                wait(act, a_qkv, t.n)
                act.copy(hh[:, :, :], hf[:, :, :]).then_inc(a_hh, 1)

            def values(t):
                wait(act, a_rope, t.n + 1)
                wait(act, a_ctx, t.n - 1)
                for b in range(2):
                    for i in range(2):
                        ins = act.copy(bdv[t.par][HD0 * i:HD0 * (i + 1), b, HD0 * i:HD0 * (i + 1)],
                                       ps[S * b:S * (b + 1), 2, QK0 - HD0:QK0])
                ins.then_inc(a_v, 1)

            def queries(t):
                wait(act, a_qkT, t.n + 1)
                wait(act, a_sc, t.n)
                act.copy(qT[:, :, :], by_feature(bank(5))).then_inc(a_qT, 1)

            def softmax_exp(t):
                wait(act, a_ds, t.n + 1)
                act.activation(ex[:, :, :, :], ex[:, :, :, :], ACT.Exp, scale=float(HD0) ** -0.5
                               ).then_inc(a_ex, 1)

            def probs_T(t):
                wait(act, a_pTr, t.n + 1)
                wait(act, a_ctx, t.n)
                act.copy(pT[:, :, :], by_feature(bank(5))).then_inc(a_pT, 1)

            def high_ctx(t):
                wait(act, a_ctx, t.n + 1)
                wait(act, a_wo, t.n)
                act.copy(by_entry(ch[:, :, :]), bank(6).rearrange("p (b j s) -> p j b s", b=2, j=KT)
                         ).then_inc(a_ch, 1)

            def square2(t):
                wait(act, a_x, t.n + 1)
                wait(act, a_x2T, t.n)
                act.activation(xn2[:, :], xt(t), ACT.Square, scale=float(D) ** -0.5,
                               accum_out=stat[:, 2, bass.ds(t.n, 1)]).then_inc(a_ssq2, 1)

            def norm2(t):
                wait(act, a_rstd2, t.n + 1)
                act.activation(xn2[:, :], xt(t), ACT.Copy, scale=stat[:, 3, bass.ds(t.n, 1)]).then_inc(a_xn2, 1)

            def high_h2(t):
                wait(act, a_gf, t.n + 1)
                act.copy(h2h[:, :, bass.ds(t.n * P, P)], gf[:, :, :]).then_inc(a_h2h, 1)

            def split_group(g, slot, reused):
                act.wait_ge(m_ld[slot], 48 * (1 + (g // 2 if isinstance(g, int) else 0)) if isinstance(g, int)
                            else (g - slot) * 24 + 48)
                if reused:
                    wait(act, m_down, (g - 1) * NBLK * TPB)
                act.copy(mwh[slot][:, :, :], mst[slot][:, :, :]).then_inc(m_wh, 1)

            def mlp_step(g, r):
                n = g * NBLK + r
                act.wait_ge(m_gate, n + 1)
                wait(act, m_af, n)
                act.activation(sg[:, :], bank(1 + r % 2), ACT.Silu).then_inc(m_sg, 1)
                act.wait_ge(m_af, n + 1)
                wait(act, m_down, TPB * (n - 1))
                wait(act, m_al, n - 1)
                act.copy(ah[r % 2][:, :], af[:, :]).then_inc(m_ah, 1)

            def mlp_group(g, slot, nxt=True):
                for r in range(NBLK):
                    mlp_step(g, r)
                    if r == 1 and nxt:
                        split_group(g + 1, 1 - slot, not (isinstance(g, int) and g == 0))

            def mlp_pairs(p_from, p_to):
                with act.Fori(p_from, p_to) as pair:
                    for k in range(2):
                        mlp_group(pair * 2 + k, k)

            run_tiles(act, NT, [(square, 3), (softmax_exp, 0), (norm, 3), (high_h, 2), (probs_T, 0),
                                (values, 1), (high_h2, -2), (square2, -1), (queries, 1), (high_ctx, 0),
                                (norm2, -1)],
                      {-2: split_qkv, -1: split_wo, X1 - 3: rest_of_x, 13: lambda: split_group(0, 0, False),
                       NT: lambda: mlp_step(0, 0), NT + 1: lambda: mlp_step(0, 1)})
            split_group(1, 1, False)
            for r in range(2, NBLK):
                mlp_step(0, r)
            mlp_group(1, 1)
            mlp_pairs(1, NG // 4)
            act.wait_ge(ld_l1, 32)
            act.copy(wqh[:, :, :], wst[:, :, :]).then_inc(w1h, 1)
            mlp_pairs(NG // 4, NG * 3 // 8)
            act.wait_ge(ld_l1, 80)
            act.copy(woh[:, :, :], wst[:, :, 0:D]).then_inc(w1h, 1)
            act.copy(kvh[:, :].rearrange("p (c n) -> p c n", c=2), wst[:, 0:2, D:D + P]).then_inc(w1h, 1)
            mlp_pairs(NG * 3 // 8, NG // 2 - 1)
            mlp_group(NG - 2, 0)
            mlp_group(NG - 1, 1, False)
            act.wait_ge(w1l, 3)

            def norm1(t):
                wait(act, b_nb, t.n + 1)
                wait(act, b_xT, t.n)
                act.activation(yn[:, :], xt(t), ACT.Identity, bias=stat[:, 5, bass.ds(t.n, 1)],
                               scale=stat[:, 4, bass.ds(t.n, 1)]).then_inc(b_xn, 1)

            def scale_shift_y(t, k_from, k_to):
                for k in range(k_from, k_to):
                    for b in range(2):
                        at = lambda tab: tab[:, k, bass.ds(t.n * 2 + b, 1)]
                        ins = act.activation(yf[:, k, S * b:S * (b + 1)],
                                             y_bank(t)[:, P * k + S * b:P * k + S * (b + 1)],
                                             ACT.Identity, bias=at(sh_ada), scale=at(sc_ada))
                return ins

            def scale_shift_lower(t):
                wait(act, b_xT, t.n + 1)
                wait(act, b_hl, t.n)
                scale_shift_y(t, 0, KT // 2)

            def scale_shift_upper(t):
                scale_shift_y(t, KT // 2, KT).then_inc(b_yf, 1)

            def high_y(t):
                wait(act, b_yf, t.n + 1)
                wait(act, b_qc, 2 * t.n)
                act.copy(yh[:, :, :], yf[:, :, :]).then_inc(b_hh, 1)

            def latent(t):
                wait(act, b_qc, 2 * t.n + 1)
                wait(act, b_latT, t.n)
                act.copy(lat[:, :], ps[:, 2, QK1 - P:QK1]).then_inc(b_lat, 1)

            def high_latent(t):
                wait(act, b_latT, t.n + 1)
                wait(act, b_kv, t.n)
                act.copy(lath[:, :], ps[:, 3, 256:384]).then_inc(b_lath, 1)

            def values1(t):
                wait(act, b_rope, t.n + 1)
                wait(act, b_ctx, t.n - 1)
                for b in range(2):
                    for i in range(2):
                        ins = act.copy(bdv1[t.par][S * i:S * (i + 1), b, :, HD1 * i:HD1 * (i + 1)],
                                       ps[S * b:S * (b + 1), 2, QK1:QK1 + P].rearrange("p (j d) -> p j d", j=KT))
                ins.then_inc(b_v, 1)

            def queries_keys1(t):
                wait(act, b_qkT, t.n + 1)
                wait(act, b_sc, t.n)
                act.copy(qk1[:, 0:2, :, :], ps[:, 3:5, 256:512].rearrange("p j (c n) -> p j c n", c=2)
                         ).then_inc(b_qka, 1)

            def softmax_exp1(t):
                for i in range(2):
                    wait(act, b_ds, 2 * t.n + i + 1)
                    half = ex1[:, :, 2 * i:2 * i + 2, :]
                    act.activation(half, half, ACT.Exp, scale=float(HD1) ** -0.5).then_inc(b_ex, 1)

            def probs_T1(t):
                wait(act, b_pTr, t.n + 1)
                wait(act, b_ctx, t.n)
                act.copy(pT1[:, 0:KT, :].rearrange("p (j i) n -> p j i n", i=2),
                         ps[:, 3:5, 256:512].rearrange("p j (i n) -> p j i n", i=2)).then_inc(b_pTa, 1)

            def high_ctx1(t):
                wait(act, b_ctx, t.n + 1)
                wait(act, b_wo, t.n)
                act.copy(yc[:, :, :], by_feature(bank(0))).then_inc(b_ch, 1)

            def values_ready():
                act.wait_ge(b_zero, 2)
                act.wait_ge(m_x, NG * NT)

            run_tiles(act, NT, [(softmax_exp1, 0), (latent, 2), (scale_shift_lower, 3), (queries_keys1, 1),
                                (scale_shift_upper, 3), (high_latent, 2), (high_y, 3), (probs_T1, 0),
                                (values1, 2), (high_ctx1, 0), (norm1, 4)],
                      {-2: values_ready})


def kernel(x, pos_BxS, cond_2048, L0_cond_ln1_w, L0_cond_ln1_tw, L0_cond_ln2_w, L0_cond_ln2_tw,
           L0_cond_Wq, L0_cond_Wk, L0_cond_Wv, L0_cond_Wo, L0_cond_Wg, L0_cond_Wu, L0_cond_Wd,
           L1_cond_W_ada, L1_cond_b_ada, L1_cond_Wq, L1_cond_Wkd, L1_cond_Wku, L1_cond_Wvu, L1_cond_Wo):
    import concourse.bacc as bacc
    from concourse.bass_utils import run_bass_kernel_spmd

    B, T, D = x.shape
    turn = lambda a: np.ascontiguousarray(np.asarray(a).T)
    column = lambda a: turn(np.asarray(a).reshape(-1, 128))
    f32 = np.float32
    hd0, hd1 = 64, 32
    invf = (f32(1.0) / np.power(f32(10000.0), np.arange(0, hd0, 2, dtype=f32) / f32(hd0))).astype(f32)
    freq1 = (f32(1.0) / np.power(f32(10000.0), np.arange(0, hd1, 2, dtype=f32) / f32(hd1))).astype(f32)
    ang1 = np.arange(T, dtype=f32)[:, None] * freq1[None, :]
    cos1, sin1 = np.cos(ang1).astype(f32), np.sin(ang1).astype(f32)
    rope1 = np.stack([np.concatenate([cos1, cos1], 1), np.concatenate([-sin1, sin1], 1)], 1)
    arrays = {
        "x": np.ascontiguousarray(np.asarray(x).reshape(B * T, D)),
        "pos": turn(np.asarray(pos_BxS).reshape(B * T // 128, 128)),
        "condT": turn(cond_2048),
        "ln1_w": column(L0_cond_ln1_w), "ln1_twT": turn(L0_cond_ln1_tw),
        "ln2_w": column(L0_cond_ln2_w), "ln2_twT": turn(L0_cond_ln2_tw),
        "WqT": turn(L0_cond_Wq), "WkT": turn(L0_cond_Wk), "WvT": turn(L0_cond_Wv), "WoT": turn(L0_cond_Wo),
        "WgT": turn(L0_cond_Wg), "WuT": turn(L0_cond_Wu), "WdT": turn(L0_cond_Wd),
        "adaT": turn(L1_cond_W_ada), "b_ada": column(L1_cond_b_ada),
        "Wq1T": turn(L1_cond_Wq), "WkdT": turn(L1_cond_Wkd), "WkuT": turn(L1_cond_Wku),
        "WvuT": turn(L1_cond_Wvu), "Wo1T": turn(L1_cond_Wo),
        "invf": np.ascontiguousarray(np.broadcast_to(invf, (128, hd0 // 2))),
        "rope1": np.ascontiguousarray(np.concatenate([rope1] * (128 // T), 0)),
        "ident": np.eye(128, dtype=f32),
    }
    nc = bacc.Bacc("TRN2", target_bir_lowering=False, num_devices=1)
    args = [nc.dram_tensor(n, a.shape, mybir.dt.from_np(a.dtype), kind="ExternalInput").ap()
            for n, a in arrays.items()]
    out = nc.dram_tensor("out", (B * T, D), F32, kind="ExternalOutput").ap()
    build(nc, *args, out)
    r = run_bass_kernel_spmd(nc, [arrays], core_ids=[0])
    return r.results[0]["out"].reshape(B, T, D)
```
